# Optimizing a Trainium2 kernel written in Bass

```python
import numpy as np
import jax
import jax.numpy as jnp

def _softmax(x, axis=-1):
    return jax.nn.softmax(x, axis=axis)

def _gelu(x):
    return jax.nn.gelu(x, approximate=True)

def _silu(x):
    return jax.nn.silu(x)

def _sigmoid(x):
    return jax.nn.sigmoid(x)

def _layernorm(x, axis=-1, eps=1e-05):
    m = jnp.mean(x, axis=axis, keepdims=True)
    v = jnp.var(x, axis=axis, keepdims=True)
    return (x - m) / jnp.sqrt(v + eps)

def _scatter_add(tgt, idx, src, axis=0):
    return tgt.at[idx].add(src)

def _segment_sum(src, seg, n):
    return jax.ops.segment_sum(src, seg, n)
kernel_name = 'mk_sandwich_d2_jaxref_r8_ec12b3'

def setup_inputs(seed: int=0):
    np.random.seed(seed)
    _w = jnp.asarray

    def _L0_attn_setup():
        import jax, jax.numpy as jnp
        import numpy as np
        HIDDEN = 256
        KEY_DIM = 256
        NUM_HEADS = 16
        HEAD_DIM = KEY_DIM // NUM_HEADS
        ROPE_THETA = 10000.0
        EPS = 1e-05

        def rms_norm(x, w, eps=EPS):
            var = jnp.mean(x * x, axis=-1, keepdims=True)
            return x * jax.lax.rsqrt(var + eps) * w

        def apply_rope(x, theta_base=ROPE_THETA):
            b, s, h, d = x.shape
            half = d // 2
            freqs = theta_base ** (jnp.arange(half, dtype=x.dtype) * (-2.0 / d))
            freqs = jnp.concatenate([freqs, freqs], axis=-1)
            pos = jnp.arange(s, dtype=x.dtype)
            ang = pos[:, None] * freqs[None, :]
            cos = jnp.cos(ang)[None, :, None, :]
            sin = jnp.sin(ang)[None, :, None, :]
            x_even = x[..., 0::2]
            x_odd = x[..., 1::2]
            x1 = jnp.concatenate([x_even, x_even], axis=-1)
            x2 = jnp.concatenate([x_odd, x_odd], axis=-1)
            even_mask = (jnp.arange(d) % 2 == 0)[None, None, None, :]
            return jnp.where(even_mask, cos * x1 - sin * x2, sin * x1 + cos * x2)
        key = jax.random.key(seed)
        ks = jax.random.split(key, 10)
        B, S = (2, 256)
        s_in = 1.0 / np.sqrt(HIDDEN)
        s_k = 1.0 / np.sqrt(KEY_DIM)
        return {'x': jax.random.normal(ks[0], (B, S, HIDDEN), dtype=jnp.float32), 'rms_w': jnp.ones((HIDDEN,), dtype=jnp.float32), 'wq': jax.random.normal(ks[1], (HIDDEN, KEY_DIM), dtype=jnp.float32) * s_in, 'bq': jnp.zeros((KEY_DIM,), dtype=jnp.float32), 'wk': jax.random.normal(ks[2], (HIDDEN, KEY_DIM), dtype=jnp.float32) * s_in, 'bk': jnp.zeros((KEY_DIM,), dtype=jnp.float32), 'wv': jax.random.normal(ks[3], (HIDDEN, KEY_DIM), dtype=jnp.float32) * s_in, 'bv': jnp.zeros((KEY_DIM,), dtype=jnp.float32), 'wo': jax.random.normal(ks[4], (KEY_DIM, HIDDEN), dtype=jnp.float32) * s_k, 'bo': jnp.zeros((HIDDEN,), dtype=jnp.float32)}
    _L0_attn_in = _L0_attn_setup()

    def _L0_ffn_setup():
        import jax, jax.numpy as jnp
        import numpy as np
        import math
        D_MODEL = 256
        D_FF = 1024
        NUM_EXPERTS = 8
        TOP_K = 2
        CAPACITY_FACTOR = 1.25
        BATCH, SEQ = (4, 256)

        def _moe_forward(x, Wg, w1, w2):
            B, T, d = x.shape
            S = B * T
            E, K = (NUM_EXPERTS, TOP_K)
            C = math.ceil(CAPACITY_FACTOR * S * K / E)
            xr = x.reshape(S, d)
            probs = jax.nn.softmax(xr @ Wg, axis=-1)
            gate_vals, expert_idx = jax.lax.top_k(probs, K)
            flat_e = expert_idx.reshape(-1)
            oh = jax.nn.one_hot(flat_e, E, dtype=jnp.int32)
            pos = jnp.sum((jnp.cumsum(oh, axis=0) - 1) * oh, axis=1)
            kept = pos < C
            i = jnp.arange(S * K)
            slot = i % K * S + i // K
            sentinel = S * K
            pos_w = jnp.where(kept, pos, C)
            dispatch_mask = jnp.full((E, C), sentinel, dtype=jnp.int32)
            dispatch_mask = dispatch_mask.at[flat_e, pos_w].set(slot.astype(jnp.int32), mode='drop')
            combine_weights = (gate_vals * kept.reshape(S, K)).T
            dispatched = xr[dispatch_mask.reshape(-1) % S].reshape(E, C, d)
            h = jax.nn.relu(jnp.einsum('ecd,edf->ecf', dispatched, w1))
            expert_out = jnp.einsum('ecf,efd->ecd', h, w2)
            rerouted = jnp.zeros((S * K + 1, d), dtype=expert_out.dtype)
            rerouted = rerouted.at[dispatch_mask.reshape(-1)].set(expert_out.reshape(-1, d))
            rerouted = rerouted[:-1].reshape(K, S, d)
            out = jnp.einsum('ks,ksm->sm', combine_weights, rerouted)
            return out.reshape(B, T, d)
        key = jax.random.key(seed)
        k1, k2, k3, k4 = jax.random.split(key, 4)
        x = jax.random.normal(k1, (BATCH, SEQ, D_MODEL), dtype=jnp.float32)
        Wg = jax.random.normal(k2, (D_MODEL, NUM_EXPERTS), dtype=jnp.float32) * 0.02
        w1 = jax.random.normal(k3, (NUM_EXPERTS, D_MODEL, D_FF), dtype=jnp.float32) * 0.02
        w2 = jax.random.normal(k4, (NUM_EXPERTS, D_FF, D_MODEL), dtype=jnp.float32) * 0.02
        return {'x': x, 'Wg': Wg, 'w1': w1, 'w2': w2}
    _L0_ffn_in = _L0_ffn_setup()

    def _L1_attn_setup():
        import jax, jax.numpy as jnp
        import numpy as np
        B, S, D, H = (2, 256, 256, 16)
        HD = D // H
        SCALE = 1.0 / np.sqrt(D).astype(np.float32)
        key = jax.random.key(seed)
        k1, k2, k3 = jax.random.split(key, 3)
        x = jax.random.normal(k1, (B, S, D), dtype=jnp.float32)
        W_qkv = jax.random.normal(k2, (3 * D, D), dtype=jnp.float32) * (1.0 / np.sqrt(D))
        W_proj = jax.random.normal(k3, (D, D), dtype=jnp.float32) * (1.0 / np.sqrt(D))
        return {'x': x, 'W_qkv': W_qkv, 'W_proj': W_proj}
    _L1_attn_in = _L1_attn_setup()

    def _L1_ffn_setup():
        import jax, jax.numpy as jnp
        import numpy as np
        N_EXPERTS = 8
        TOP_K = 2
        C = 256
        H = 128
        HS = 256
        B, T = (1, 64)
        SCALE = 0.02
        key = jax.random.key(seed)
        ks = jax.random.split(key, 10)
        x = jax.random.normal(ks[0], (B, T, C), dtype=jnp.float32)
        gate_w = jax.random.normal(ks[1], (N_EXPERTS, C), dtype=jnp.float32) * SCALE
        w_gate = jax.random.normal(ks[2], (N_EXPERTS, H, C), dtype=jnp.float32) * SCALE
        w_up = jax.random.normal(ks[3], (N_EXPERTS, H, C), dtype=jnp.float32) * SCALE
        w_down = jax.random.normal(ks[4], (N_EXPERTS, C, H), dtype=jnp.float32) * SCALE
        sh_gate = jax.random.normal(ks[5], (HS, C), dtype=jnp.float32) * SCALE
        sh_up = jax.random.normal(ks[6], (HS, C), dtype=jnp.float32) * SCALE
        sh_down = jax.random.normal(ks[7], (C, HS), dtype=jnp.float32) * SCALE
        se_gate_w = jax.random.normal(ks[8], (1, C), dtype=jnp.float32) * SCALE
        return {'x': x, 'gate_w': gate_w, 'w_gate': w_gate, 'w_up': w_up, 'w_down': w_down, 'sh_gate': sh_gate, 'sh_up': sh_up, 'sh_down': sh_down, 'se_gate_w': se_gate_w}
    _L1_ffn_in = _L1_ffn_setup()
    _d = {'L0_attn_x': _L0_attn_in['x'], 'L0_attn_rms_w': _L0_attn_in['rms_w'], 'L0_attn_wq': _L0_attn_in['wq'], 'L0_attn_bq': _L0_attn_in['bq'], 'L0_attn_wk': _L0_attn_in['wk'], 'L0_attn_bk': _L0_attn_in['bk'], 'L0_attn_wv': _L0_attn_in['wv'], 'L0_attn_bv': _L0_attn_in['bv'], 'L0_attn_wo': _L0_attn_in['wo'], 'L0_attn_bo': _L0_attn_in['bo'], 'L0_ffn_Wg': _L0_ffn_in['Wg'], 'L0_ffn_w1': _L0_ffn_in['w1'], 'L0_ffn_w2': _L0_ffn_in['w2'], 'L1_attn_W_qkv': _L1_attn_in['W_qkv'], 'L1_attn_W_proj': _L1_attn_in['W_proj'], 'L1_ffn_gate_w': _L1_ffn_in['gate_w'], 'L1_ffn_w_gate': _L1_ffn_in['w_gate'], 'L1_ffn_w_up': _L1_ffn_in['w_up'], 'L1_ffn_w_down': _L1_ffn_in['w_down'], 'L1_ffn_sh_gate': _L1_ffn_in['sh_gate'], 'L1_ffn_sh_up': _L1_ffn_in['sh_up'], 'L1_ffn_sh_down': _L1_ffn_in['sh_down'], 'L1_ffn_se_gate_w': _L1_ffn_in['se_gate_w']}
    _x0 = _d['L0_attn_x']
    _d['L0_attn_x'] = jax.random.normal(jax.random.fold_in(jax.random.key(seed), 1), (4, 512, 256), dtype=_x0.dtype)
    del _x0
    return _d

def reference(L0_attn_x, L0_attn_rms_w, L0_attn_wq, L0_attn_bq, L0_attn_wk, L0_attn_bk, L0_attn_wv, L0_attn_bv, L0_attn_wo, L0_attn_bo, L0_ffn_Wg, L0_ffn_w1, L0_ffn_w2, L1_attn_W_qkv, L1_attn_W_proj, L1_ffn_gate_w, L1_ffn_w_gate, L1_ffn_w_up, L1_ffn_w_down, L1_ffn_sh_gate, L1_ffn_sh_up, L1_ffn_sh_down, L1_ffn_se_gate_w):

    def _L0_attn_ref(x, rms_w, wq, bq, wk, bk, wv, bv, wo, bo):
        import jax, jax.numpy as jnp
        import numpy as np
        HIDDEN = 256
        KEY_DIM = 256
        NUM_HEADS = 16
        HEAD_DIM = KEY_DIM // NUM_HEADS
        ROPE_THETA = 10000.0
        EPS = 1e-05

        def rms_norm(x, w, eps=EPS):
            var = jnp.mean(x * x, axis=-1, keepdims=True)
            return x * jax.lax.rsqrt(var + eps) * w

        def apply_rope(x, theta_base=ROPE_THETA):
            b, s, h, d = x.shape
            half = d // 2
            freqs = theta_base ** (jnp.arange(half, dtype=x.dtype) * (-2.0 / d))
            freqs = jnp.concatenate([freqs, freqs], axis=-1)
            pos = jnp.arange(s, dtype=x.dtype)
            ang = pos[:, None] * freqs[None, :]
            cos = jnp.cos(ang)[None, :, None, :]
            sin = jnp.sin(ang)[None, :, None, :]
            x_even = x[..., 0::2]
            x_odd = x[..., 1::2]
            x1 = jnp.concatenate([x_even, x_even], axis=-1)
            x2 = jnp.concatenate([x_odd, x_odd], axis=-1)
            even_mask = (jnp.arange(d) % 2 == 0)[None, None, None, :]
            return jnp.where(even_mask, cos * x1 - sin * x2, sin * x1 + cos * x2)
        B, S, _ = x.shape
        residual = x
        xn = rms_norm(x, rms_w)
        q = (xn @ wq + bq).reshape(B, S, NUM_HEADS, HEAD_DIM)
        k = (xn @ wk + bk).reshape(B, S, NUM_HEADS, HEAD_DIM)
        v = (xn @ wv + bv).reshape(B, S, NUM_HEADS, HEAD_DIM)
        q = apply_rope(q)
        k = apply_rope(k)
        scores = jnp.einsum('bshd,bthd->bhst', q, k) / jnp.sqrt(jnp.asarray(HEAD_DIM, dtype=x.dtype))
        causal = jnp.tril(jnp.ones((S, S), dtype=bool))[None, None]
        scores = jnp.where(causal, scores, -jnp.inf)
        probs = jax.nn.softmax(scores, axis=-1)
        out = jnp.einsum('bhst,bthd->bshd', probs, v).reshape(B, S, KEY_DIM)
        return out @ wo + bo + residual

    def _L0_ffn_ref(x, Wg, w1, w2):
        import jax, jax.numpy as jnp
        import numpy as np
        import math
        D_MODEL = 256
        D_FF = 1024
        NUM_EXPERTS = 8
        TOP_K = 2
        CAPACITY_FACTOR = 1.25
        BATCH, SEQ = (4, 256)

        def _moe_forward(x, Wg, w1, w2):
            B, T, d = x.shape
            S = B * T
            E, K = (NUM_EXPERTS, TOP_K)
            C = math.ceil(CAPACITY_FACTOR * S * K / E)
            xr = x.reshape(S, d)
            probs = jax.nn.softmax(xr @ Wg, axis=-1)
            gate_vals, expert_idx = jax.lax.top_k(probs, K)
            flat_e = expert_idx.reshape(-1)
            oh = jax.nn.one_hot(flat_e, E, dtype=jnp.int32)
            pos = jnp.sum((jnp.cumsum(oh, axis=0) - 1) * oh, axis=1)
            kept = pos < C
            i = jnp.arange(S * K)
            slot = i % K * S + i // K
            sentinel = S * K
            pos_w = jnp.where(kept, pos, C)
            dispatch_mask = jnp.full((E, C), sentinel, dtype=jnp.int32)
            dispatch_mask = dispatch_mask.at[flat_e, pos_w].set(slot.astype(jnp.int32), mode='drop')
            combine_weights = (gate_vals * kept.reshape(S, K)).T
            dispatched = xr[dispatch_mask.reshape(-1) % S].reshape(E, C, d)
            h = jax.nn.relu(jnp.einsum('ecd,edf->ecf', dispatched, w1))
            expert_out = jnp.einsum('ecf,efd->ecd', h, w2)
            rerouted = jnp.zeros((S * K + 1, d), dtype=expert_out.dtype)
            rerouted = rerouted.at[dispatch_mask.reshape(-1)].set(expert_out.reshape(-1, d))
            rerouted = rerouted[:-1].reshape(K, S, d)
            out = jnp.einsum('ks,ksm->sm', combine_weights, rerouted)
            return out.reshape(B, T, d)
        return _moe_forward(x, Wg, w1, w2)

    def _L1_attn_ref(x, W_qkv, W_proj):
        import jax, jax.numpy as jnp
        import numpy as np
        B, S, D, H = (2, 256, 256, 16)
        HD = D // H
        SCALE = 1.0 / np.sqrt(D).astype(np.float32)
        b, s, d = x.shape
        qkv = x @ W_qkv.T
        q, k, v = jnp.split(qkv, 3, axis=-1)
        q = q.reshape(b, s, H, HD).transpose(0, 2, 1, 3)
        k = k.reshape(b, s, H, HD).transpose(0, 2, 1, 3)
        v = v.reshape(b, s, H, HD).transpose(0, 2, 1, 3)
        attn = jnp.einsum('bhqd,bhkd->bhqk', q, k) * SCALE
        causal = jnp.tril(jnp.ones((s, s), dtype=bool))
        attn = jnp.where(causal[None, None], attn, -jnp.inf)
        probs = jax.nn.softmax(attn, axis=-1)
        out = jnp.einsum('bhqk,bhkd->bhqd', probs, v)
        out = out.transpose(0, 2, 1, 3).reshape(b, s, d)
        return out @ W_proj.T

    def _L1_ffn_ref(x, gate_w, w_gate, w_up, w_down, sh_gate, sh_up, sh_down, se_gate_w):
        import jax, jax.numpy as jnp
        import numpy as np
        N_EXPERTS = 8
        TOP_K = 2
        C = 256
        H = 128
        HS = 256
        B, T = (1, 64)
        SCALE = 0.02
        Bb, Tt, Cc = x.shape
        xf = x.reshape(-1, Cc)
        scores = xf @ gate_w.T
        ew, ei = jax.lax.top_k(scores, TOP_K)
        ew = jax.nn.softmax(ew, axis=-1)
        x1 = jax.nn.silu(jnp.einsum('td,ehd->teh', xf, w_gate))
        x3 = jnp.einsum('td,ehd->teh', xf, w_up)
        expert_out = jnp.einsum('teh,edh->ted', x1 * x3, w_down)
        onehot = jax.nn.one_hot(ei, N_EXPERTS, dtype=ew.dtype)
        comb = jnp.einsum('ta,tae->te', ew, onehot)
        routed = jnp.einsum('te,ted->td', comb, expert_out)
        shared = jax.nn.silu(xf @ sh_gate.T) * (xf @ sh_up.T) @ sh_down.T
        sgate = jax.nn.sigmoid(xf @ se_gate_w.T)
        return (routed + sgate * shared).reshape(Bb, Tt, Cc)
    x = L0_attn_x
    x = x + _layernorm(_L0_attn_ref(_layernorm(x, axis=-1), L0_attn_rms_w, L0_attn_wq, L0_attn_bq, L0_attn_wk, L0_attn_bk, L0_attn_wv, L0_attn_bv, L0_attn_wo, L0_attn_bo), axis=-1)
    x = x + _layernorm(_L0_ffn_ref(_layernorm(x, axis=-1), L0_ffn_Wg, L0_ffn_w1, L0_ffn_w2), axis=-1)
    x = x + _layernorm(_L1_attn_ref(_layernorm(x, axis=-1), L1_attn_W_qkv, L1_attn_W_proj), axis=-1)
    x = x + _layernorm(_L1_ffn_ref(_layernorm(x, axis=-1), L1_ffn_gate_w, L1_ffn_w_gate, L1_ffn_w_up, L1_ffn_w_down, L1_ffn_sh_gate, L1_ffn_sh_up, L1_ffn_sh_down, L1_ffn_se_gate_w), axis=-1)
    return x

_drawn_inputs = setup_inputs


def setup_inputs(seed=0):
    import zlib

    import numpy as np

    out = dict(_drawn_inputs(seed))
    spreads = {'L0_attn_rms_w': (1.0, 0.2),
     'L0_attn_bq': (0.0, 0.1),
     'L0_attn_bk': (0.0, 0.1),
     'L0_attn_bv': (0.0, 0.1),
     'L0_attn_bo': (0.0, 0.1)}
    factors = {}
    for name, (base, spread) in spreads.items():
        noise = np.random.default_rng([zlib.crc32(name.encode()), seed]).standard_normal(out[name].shape)
        drawn = base * np.exp(spread * noise) if base else spread * noise
        out[name] = jnp.asarray(drawn.astype(out[name].dtype))
    for name, factor in factors.items():
        out[name] = (out[name] * factor).astype(out[name].dtype)
    return out
```

```python
from contextlib import ExitStack

import numpy as np

import concourse.bass as bass
from concourse import mybir

F32 = mybir.dt.float32
BF16 = mybir.dt.bfloat16
I32 = mybir.dt.int32
U32 = mybir.dt.uint32
ALU = mybir.AluOpType
ACT = mybir.ActivationFunctionType
AX_X = mybir.AxisListType.X

P = 128
BATCH, SEQ, D = 4, 512, 256
HEADS, HD = 16, 16
KC = D // P
TPB = SEQ // P
TILES = BATCH * TPB
PADT = TPB
XT = TILES + 2 * PADT
GROUPS = 4
HPG = HEADS // GROUPS
STEPS = BATCH * GROUPS
EPS = 1e-5
NEG = -1e38
PIECES = 3
Q_STACK = (0, 0, 0, 1, 1, 2)
K_STACK = (0, 1, 2, 0, 1, 0)
SROWS = len(Q_STACK) * HD
VW = 32
UNITS = 10

E0, FF, CAP = 8, 1024, 640
FC = FF // P
CT = CAP // P
SLOTS = E0 * CAP
E1, H1 = 8, 128
HB = E1 + 2


def held(eng, gate, on, value):
    eng.wait_ge(on, value)
    eng.sem_inc(gate, 1)


class Joining:

    def __init__(self, nc, ctx, keep, tag, then_stats=True):
        self.nc, self.keep, self.then_stats = nc, keep, then_stats
        sb = lambda n, shape: ctx.enter_context(nc.sbuf_tensor(f"{tag}_{n}", shape, F32))
        sem = lambda n: ctx.enter_context(nc.semaphore(f"{tag}_{n}"))
        self.stats, self.moments = sb("stats", [P, TPB, 6]), sb("moments", [P, 2, TPB, 2])
        self.var_eps, self.inv = sb("var_eps", [P, 2, TPB]), sb("inv", [P, TPB])
        self.minus_half = sb("minus_half", [P, 1])
        self.norm_chain, self.var_ready, self.root_ready, self.joined = (
            sem("norm_chain"), sem("var_ready"), sem("root_ready"), sem("joined"))
        self.half_ready, self.gate = sem("half_ready"), sem("gate")
        self.CHAIN = 7 if then_stats else 4
        self.VARS = 2 if then_stats else 1

    def stats_of(self, src, n0, i, chain=False):
        ins = self.nc.vector.bn_stats(self.stats[:, i, :],
                                      src[:, bass.ds(n0 + i, 1), :].rearrange("p a d -> p (a d)"))
        if i == TPB - 1:
            ins.then_inc(self.norm_chain, 1)

    def variance(self, dve, which, k, c):
        nc = self.nc
        held(dve, self.gate, self.norm_chain, k * self.CHAIN + c)
        for i in range(TPB):
            last = nc.vector.bn_aggr(self.moments[:, which, i, :], self.stats[:, i, :])
        last.then_inc(self.norm_chain, 1)
        dve.wait_ge(self.norm_chain, k * self.CHAIN + (c + 1))
        nc.vector.tensor_scalar(self.var_eps[:, which, :], self.moments[:, which, :, 1], EPS, None,
                                ALU.add).then_inc(self.var_ready, 1)

    def sub_variance(self, dve, k):
        self.variance(dve, 0, k, 1)

    def normalise_tile(self, dve, k, n0, i):
        sub = self.keep["sub"]
        tile = sub[:, bass.ds(n0 + i, 1), :].rearrange("p a d -> p (a d)")
        if i == 0:
            dve.wait_ge(self.root_ready, k * self.VARS + 1)
        ins = self.nc.vector.tensor_scalar(tile, tile, self.moments[:, 0, i, 0:1], self.inv[:, i:i + 1],
                                           ALU.subtract, ALU.mult)
        if i == TPB - 1:
            ins.then_inc(self.norm_chain, 1)

    def add(self, dve, k, n0):
        x, sub = self.keep["x"], self.keep["sub"]
        dve.wait_ge(self.norm_chain, k * self.CHAIN + 3)
        self.nc.vector.tensor_tensor(x[:, bass.ds(n0, TPB), :], x[:, bass.ds(n0, TPB), :],
                                     sub[:, bass.ds(n0, TPB), :], ALU.add).then_inc(self.norm_chain, 1)
        dve.wait_ge(self.norm_chain, k * self.CHAIN + 4)
        dve.sem_inc(self.joined, 1)

    def x_variance(self, dve, k, n0):
        self.variance(dve, 1, k, 5)
        self.nc.vector.tensor_copy(self.keep["mean"][:, bass.ds(n0, TPB)],
                                   self.moments[:, 1, :, 0]).then_inc(self.norm_chain, 1)

    def all_on_vector(self, dve, k, n0):
        for i in range(TPB):
            self.stats_of(self.keep["sub"], n0, i)
        self.sub_variance(dve, k)
        for i in range(TPB):
            self.normalise_tile(dve, k, n0, i)
        self.add(dve, k, n0)
        if self.then_stats:
            for i in range(TPB):
                self.stats_of(self.keep["x"], n0, i)
            self.x_variance(dve, k, n0)

    def start_pool(self, pool):
        self.nc.gpsimd.memset(self.minus_half[:, :], -0.5).then_inc(self.half_ready, 1)
        pool.wait_ge(self.half_ready, 1)

    def sub_root(self, pool, gate, k):
        held(pool, gate, self.var_ready, k * self.VARS + 1)
        self.nc.gpsimd.tensor_tensor(self.inv[:, :], self.var_eps[:, 0, :],
                                     self.minus_half[:, :].to_broadcast([P, TPB]), ALU.pow)\
            .then_inc(self.root_ready, 1)

    def x_root(self, pool, gate, k, n0):
        held(pool, gate, self.var_ready, k * 2 + 2)
        for name in ("rstd", "rin"):
            last = self.nc.gpsimd.tensor_tensor(self.keep[name][:, bass.ds(n0, TPB)], self.var_eps[:, 1, :],
                                                self.minus_half[:, :].to_broadcast([P, TPB]), ALU.pow)
        last.then_inc(self.root_ready, 1)


def attention_phase(nc, keep, w, layer):
    rope = layer == 0
    scale = float(HD) ** -0.5 if rope else float(D) ** -0.5
    x, sub, mean, rstd, rin = keep["x"], keep["sub"], keep["mean"], keep["rstd"], keep["rin"]
    ident, identb, mask_q, mask_k = keep["ident"], keep["identb"], keep["mask_q"], keep["mask_k"]
    RUNS = (((0, 3, 0, 0), (3, 2, 1, 0), (5, 1, 2, 0)), ((0, 3, 0, 1), (3, 2, 0, 1), (5, 1, 0, 0)))
    OUT_INC, STACK_INC = 16 * 6, 16 * 2
    with ExitStack() as ctx:
        def sb(name, shape, dt=F32):
            return ctx.enter_context(nc.sbuf_tensor(f"a{layer}_{name}", shape, dt))

        def psum(name, shape, dt=F32):
            return ctx.enter_context(nc.psum_tensor(f"a{layer}_{name}", shape, dt))

        def sem(name):
            return ctx.enter_context(nc.semaphore(f"a{layer}_{name}"))

        w_x1 = sb("w_x1", [P, KC, GROUPS, P])
        w_v = sb("w_v", [P, KC, D])
        w_o = sb("w_o", [P, KC, D])
        if rope:
            w_x2 = sb("w_x2", [P, KC, GROUPS, P])
            bias1, bias2 = sb("bias1", [P, GROUPS]), sb("bias2", [P, GROUPS])
            bias_v, bias_o = sb("bias_v", [P, D]), sb("bias_o", [P, D])
            rms_w = sb("rms_w", [P, KC])
            rot1, rot2 = sb("rot1", [P, SEQ]), sb("rot2", [P, SEQ])
            part2 = sb("part2", [P, SEQ])
            resid = sb("resid", [P, 2, D])
        part1 = sb("part1", [P, SEQ])
        y_tok = sb("y_tok", [P, TPB, D])
        y_t = sb("y_t", [P, KC, SEQ])
        qk = sb("qk", [P, SEQ]) if rope else part1
        rest1 = sb("rest1", [P, SEQ])
        pieces = sb("pieces", [P, PIECES, SEQ], BF16)
        q_st = [sb(f"q_st{g}", [P, HPG, SEQ], BF16) for g in range(GROUPS)]
        k_st = [sb(f"k_st{g}", [P, HPG, SEQ], BF16) for g in range(GROUPS)]
        v = sb("v", [P, TPB, HEADS, VW])
        probs = sb("probs", [P, UNITS, SEQ])
        nmax = sb("nmax", [P, TPB, HPG])
        nrest = sb("nrest", [P, TPB, HPG])
        nmax_p = sb("nmax_p", [P, TPB, HPG, PIECES], BF16)
        pv_sb = sb("pv_sb", [P, SEQ])
        rsum = sb("rsum", [P, TPB, HPG])
        o_tok = sb("o_tok", [P, TPB, D])
        o_t = sb("o_t", [P, KC, SEQ])

        ps_a = [psum(f"ps_a{i}", [P, SEQ]) for i in range(2)]
        ps_b = [psum(f"ps_b{i}", [P, SEQ]) for i in range(2)]
        ps_pv = psum("ps_pv", [P, SEQ])
        ps_x1 = psum("ps_x1", [P, SEQ])
        ps_x2 = psum("ps_x2", [P, SEQ])
        ps_m = psum("ps_m", [P, SEQ])

        weights_in = sem("weights_in")
        v_const = sem("v_const")
        y_ready = sem("y_ready")
        x1_full, x1_free = sem("x1_full"), sem("x1_free")
        x2_full, x2_free = sem("x2_full"), sem("x2_free")
        m_full, m_free = sem("m_full"), sem("m_free")
        pool_chain = sem("pool_chain")
        dve_chain = sem("dve_chain")
        pieces_out = sem("pieces_out")
        stacked = sem("stacked")
        a_full, maxes = sem("a_full"), sem("maxes")
        b_full, exps = sem("b_full"), sem("exps")
        nmax_ready, copies = sem("nmax_ready"), sem("copies")
        pv_done, pv_copied = sem("pv_done"), sem("pv_copied")
        rsum_ready = sem("rsum_ready")
        out_chain = sem("out_chain")
        init_done = sem("init_done")

        scratch = w["scratch"]

        AHEAD = 3
        M_PRO, M_PER = KC, 16
        M_AT = {}
        n = 0
        for g in range(GROUPS):
            uses = ["max"]
            if g == 0:
                uses += ["v0", "v1"]
            if g == 1:
                uses += ["ot0", "ot1", "out0", "out1"]
            uses += ["o"]
            if g == 0:
                uses += ["yt0", "yt1"]
            for u in uses:
                M_AT[(g, u)] = n
                n += 1
        assert n == M_PER

        def m_use(b, g, u):
            return b * M_PER + (M_PRO + M_AT[(g, u)])

        def x2_proj(t):
            return t if isinstance(t, int) else t * 2 - (AHEAD - 1)

        def x2_max(t):
            return t * 2 + AHEAD if rope else t

        POOL_PER = 3 if rope else 2

        gate = sem("gate")
        join = Joining(nc, ctx, keep, f"a{layer}_join")

        block = ctx.enter_context(nc.Block())

        @block.sync
        def _(sp):
            loads = [(w_x1[:, :, :, :], w["x1"]), (w_v[:, :, :], w["v"]), (w_o[:, :, :], w["o"])]
            if rope:
                loads += [(w_x2[:, :, :, :], w["x2"]), (bias1[:, :], w["bias1"]), (bias2[:, :], w["bias2"]),
                          (bias_v[:, :], w["bias_v"]), (bias_o[:, :], w["bias_o"]), (rms_w[:, :], w["rms_w"]),
                          (rot1[:, :], w["rot1"]), (rot2[:, :], w["rot2"])]
            for dst, src in loads:
                sp.dma_start(dst, src).then_inc(weights_in, 16)

            def restack(b, g, ahead):
                t = b * GROUPS + (g + ahead)
                slot = (g + ahead) % GROUPS
                held(sp, gate, pool_chain, t * POOL_PER + POOL_PER)
                for half, runs in enumerate(RUNS):
                    rows = slice(half * HPG * HD, (half + 1) * HPG * HD)
                    for r, n, i, step in runs:
                        src = pieces[rows, i:i + n, :] if step else pieces[rows, i:i + 1, :].to_broadcast(
                            [HPG * HD, n, SEQ])
                        sp.dma_start(scratch[slot % 2, half, r:r + n].rearrange("r d h s -> (d h) r s"), src)\
                          .then_inc(pieces_out, 16)
                held(sp, gate, pieces_out, t * OUT_INC + OUT_INC)
                if ahead == AHEAD:
                    held(sp, gate, pv_done, b * GROUPS + (g + 2))
                for half, st in enumerate((q_st[slot], k_st[slot])):
                    sp.dma_start(st[0:SROWS, :, :], scratch[slot % 2, half].rearrange("r d h s -> (r d) h s"))\
                      .then_inc(stacked, 16)
                held(sp, gate, stacked, t * STACK_INC + STACK_INC)

            for ahead in range(AHEAD):
                restack(0, 0, ahead)
            with sp.Fori(0, BATCH) as b:
                for g in range(GROUPS):
                    restack(b, g, AHEAD)

        @block.gpsimd
        def _(pool):
            def split(b, g, ahead):
                t = b * GROUPS + (g + ahead)
                c = t * POOL_PER
                if rope:
                    held(pool, gate, x1_free, t + 2)
                    held(pool, gate, x2_free, x2_proj(t) + 2)
                    nc.gpsimd.tensor_tensor(qk[:, :], part1[:, :], part2[:, :], ALU.add).then_inc(pool_chain, 1)
                held(pool, gate, copies, t * 2 + 1)
                nc.gpsimd.tensor_tensor(rest1[:, :], qk[:, :], pieces[:, 0, :], ALU.subtract).then_inc(pool_chain, 1)
                held(pool, gate, copies, t * 2 + 2)
                nc.gpsimd.tensor_tensor(pieces[:, 2, :], rest1[:, :], pieces[:, 1, :],
                                        ALU.subtract).then_inc(pool_chain, 1)

            join.start_pool(pool)
            for ahead in range(AHEAD):
                split(0, 0, ahead)
            with pool.Fori(0, BATCH) as b:
                for g in range(GROUPS):
                    if g == 2:
                        join.sub_root(pool, gate, b)
                    split(b, g, AHEAD)
                    if g == 3:
                        join.x_root(pool, gate, b, b * TPB)
            join.sub_root(pool, gate, BATCH)
            join.x_root(pool, gate, BATCH, BATCH * TPB)

        @block.scalar
        def _(act):
            act.sem_inc(exps, 2)
            act.sem_inc(pv_copied, 1)
            act.sem_inc(m_free, 1)
            if not rope:
                act.sem_inc(x1_free, 1)

            def y_evac(use, c):
                act.wait_ge(m_full, use + 1)
                if rope:
                    nc.scalar.mul(y_t[:, c, :], ps_m[:, :], rms_w[:, c:c + 1]).then_inc(m_free, 1)
                else:
                    nc.scalar.copy(y_t[:, c, :], ps_m[:, :]).then_inc(m_free, 1)

            def rows_evac(use, slot):
                act.wait_ge(m_full, use + 1)
                nc.scalar.copy(q_st[slot][SROWS:SROWS + PIECES, 0:2, :],
                               ps_m[:, :].bitcast(BF16)[SROWS:SROWS + PIECES, :].rearrange(
                                   "p (h s) -> p h s", h=2)).then_inc(m_free, 1)

            def first_part(t):
                if rope:
                    act.wait_ge(pool_chain, t * POOL_PER + 1)
                else:
                    act.wait_ge(x1_free, t + 2)
                if not isinstance(t, int) or t > 0:
                    act.wait_ge(pieces_out, t * OUT_INC)
                nc.scalar.copy(pieces[:, 0, :], qk[:, :]).then_inc(copies, 1)

            def second_part(t):
                act.wait_ge(pool_chain, t * POOL_PER + (POOL_PER - 1))
                nc.scalar.copy(pieces[:, 1, :], rest1[:, :]).then_inc(copies, 1)

            def x1_evac(t):
                act.wait_ge(x1_full, t + 1)
                if not isinstance(t, int) or t > 0:
                    act.wait_ge(pool_chain, t * POOL_PER)
                nc.scalar.copy(part1[:, :], ps_x1[:, :]).then_inc(x1_free, 1)

            def ot_evac(use, c):
                act.wait_ge(m_full, use + 1)
                nc.scalar.copy(o_t[:, c, :], ps_m[:, :]).then_inc(m_free, 1)

            if rope:
                act.wait_ge(weights_in, 16 * 11)
            for c in range(KC):
                y_evac(c, c)
            for t in range(AHEAD):
                if not rope:
                    x1_evac(t)
                first_part(t)
                second_part(t)
            with act.Fori(0, BATCH) as b:
                for g in range(GROUPS):
                    t = b * GROUPS + g
                    rows_evac(m_use(b, g, "max"), g)
                    if g == 0 and not rope:
                        for i in range(2):
                            act.wait_ge(m_full, m_use(b, 0, f"v{i}") + 1)
                            nc.scalar.copy(v[:, 2 * i:2 * i + 2, :, 0:HD],
                                           ps_m[:, :].rearrange("p (i h d) -> p i h d", i=2, d=HD)).then_inc(m_free, 1)
                    if not rope:
                        x1_evac(t + AHEAD)
                    if g == 1:
                        for c in range(KC):
                            ot_evac(m_use(b, 1, f"ot{c}"), c)
                    for k in range(UNITS):
                        act.wait_ge(b_full, t * UNITS + (k + 1))
                        if k == 0:
                            act.wait_ge(pv_done, t + 2)
                        nc.scalar.activation(probs[:, k, :], ps_b[k % 2][:, :], ACT.Exp,
                                             scale=scale).then_inc(exps, 1)
                        if k == 1:
                            first_part(t + AHEAD)
                        if k == 4:
                            second_part(t + AHEAD)
                    act.wait_ge(pv_done, t + 3)
                    act.wait_ge(m_full, m_use(b, g, "o") + 1)
                    nc.scalar.copy(pv_sb[:, :], ps_pv[:, :]).then_inc(pv_copied, 1)
                    if g == 0:
                        for c in range(KC):
                            y_evac(m_use(b, 0, f"yt{c}"), c)
            for c in range(KC):
                ot_evac(BATCH * M_PER + M_PRO + 1 + c, c)

        @block.tensor
        def _(pe):
            pe.sem_inc(pv_done, 2)

            def y_transposes(use, b1, c):
                pe.wait_ge(y_ready, b1 * TPB + TPB)
                pe.wait_ge(m_free, use + 1)
                for i in range(TPB):
                    last = nc.tensor.transpose(ps_m[:, i * P:(i + 1) * P], y_tok[:, i, c * P:(c + 1) * P], ident[:, :])
                last.then_inc(m_full, 1)

            def project(t, g, y_uses):
                pe.wait_ge(m_free, y_uses + 2)
                banks = ((w_x1, ps_x1, x1_full, x1_free, t), (w_x2, ps_x2, x2_full, x2_free, x2_proj(t))) \
                    if rope else ((w_x1, ps_x1, x1_full, x1_free, t),)
                for wt, ps, full, free, use in banks:
                    pe.wait_ge(free, use + 1)
                    for c in range(KC):
                        last = nc.tensor.matmul(ps[:, :], wt[:, c, g, :], y_t[:, c, :],
                                                start=(c == 0), stop=(c == KC - 1))
                    last.then_inc(full, 1)

            def mask(ps, lo, m):
                return nc.tensor.matmul(ps[:, lo:lo + P], identb[:, :], m[:, :], start=False, stop=True)

            def max_unit(t, slot, k):
                ps = ps_a[k % 2]
                pe.wait_ge(maxes, t * UNITS + (k + 1))
                if k < 4:
                    work = [(k, 3, 0)]
                elif k < 8:
                    work = [(k - 4, 2, 0), (k - 4, 0, 3 * P)]
                else:
                    work = [(2 * (k - 8), 1, 0), (2 * (k - 8) + 1, 1, 2 * P)]
                for h, i, at in work:
                    wd = (i + 1) * P
                    nc.tensor.matmul(ps[:, at:at + wd], q_st[slot][0:SROWS, h, i * P:(i + 1) * P],
                                     k_st[slot][0:SROWS, h, 0:wd], start=True, stop=False)
                    last = mask(ps, at + i * P, mask_q)
                last.then_inc(a_full, 1)

            def prob_unit(t, slot, k):
                ps = ps_b[k % 2]
                pe.wait_ge(exps, t * UNITS + (k + 1))
                if k < 4:
                    work = [(k, 0, 0)]
                elif k < 8:
                    work = [(k - 4, 1, 0), (k - 4, 3, 3 * P)]
                else:
                    work = [(2 * (k - 8), 2, 0), (2 * (k - 8) + 1, 2, 2 * P)]
                for h, j, at in work:
                    wd = SEQ - j * P
                    nc.tensor.matmul(ps[:, at:at + wd], k_st[slot][0:SROWS + PIECES, h, j * P:(j + 1) * P],
                                     q_st[slot][0:SROWS + PIECES, h, j * P:SEQ], start=True, stop=False)
                    last = mask(ps, at, mask_k)
                last.then_inc(b_full, 1)

            def pv(g, j):
                for h in range(HPG):
                    lo = j * P
                    rhs = {0: probs[:, h, :], 1: probs[:, 4 + h, 0:3 * P], 3: probs[:, 4 + h, 3 * P:SEQ],
                           2: probs[:, 8 + h // 2, (h % 2) * 2 * P:(h % 2) * 2 * P + 2 * P]}[j]
                    last = nc.tensor.matmul(ps_pv[h * VW:(h + 1) * VW, lo:SEQ], v[:, j, g * HPG + h, :], rhs,
                                            start=(j == 0), stop=(j == 2), skip_group_check=True)
                return last

            def max_transposes(t, use):
                pe.wait_ge(nmax_ready, t + 1)
                for ps, full, free, n in ((ps_m, m_full, m_free, use), (ps_x2, x2_full, x2_free, x2_max(t))):
                    pe.wait_ge(free, n + 1)
                    rows = ps[:, :].bitcast(BF16)[SROWS:SROWS + PIECES, :]
                    for h in range(2):
                        for i in range(TPB):
                            last = nc.tensor.transpose(rows[:, h * SEQ + i * P:h * SEQ + (i + 1) * P],
                                                       nmax_p[:, i, h + (0 if ps is ps_m else 2), :], identb[:, :])
                    last.then_inc(full, 1)

            def o_transposes(use, copied):
                pe.wait_ge(pv_copied, copied)
                pe.wait_ge(m_free, use + 1)
                for i in range(TPB):
                    last = nc.tensor.transpose(ps_m[:, i * P:(i + 1) * P], pv_sb[:, i * P:(i + 1) * P], ident[:, :])
                last.then_inc(m_full, 1)

            def o_project(use, o_done):
                pe.wait_ge(m_free, o_done)
                for c in range(KC):
                    pe.wait_ge(m_free, use + (c + 1))
                    for i in range(TPB):
                        last = nc.tensor.transpose(ps_m[:, i * P:(i + 1) * P], o_tok[:, i, c * P:(c + 1) * P],
                                                   ident[:, :])
                    last.then_inc(m_full, 1)
                for i in range(TPB):
                    if i % 2 == 0:
                        pe.wait_ge(m_free, use + (3 + i // 2))
                    for c in range(KC):
                        last = nc.tensor.matmul(ps_m[:, (i % 2) * D:(i % 2 + 1) * D], o_t[:, c, i * P:(i + 1) * P],
                                                w_o[:, c, :], start=(c == 0), stop=(c == KC - 1))
                    if i % 2:
                        last.then_inc(m_full, 1)

            pe.wait_ge(weights_in, 16 * (11 if rope else 3))
            for c in range(KC):
                y_transposes(c, 0, c)
            for ahead in range(AHEAD):
                project(ahead, ahead, KC - 1)
            pe.wait_ge(stacked, STACK_INC)
            for k in range(UNITS):
                max_unit(0, 0, k)
            pe.wait_ge(v_const, GROUPS + 3)
            with pe.Fori(0, BATCH) as b:
                for g in range(GROUPS):
                    t = b * GROUPS + g
                    max_transposes(t, m_use(b, g, "max"))
                    if g == 0:
                        for i in range(TPB):
                            if i % 2 == 0:
                                pe.wait_ge(m_free, m_use(b, 0, f"v{i // 2}") + 1)
                            for c in range(KC):
                                last = nc.tensor.matmul(ps_m[:, (i % 2) * D:(i % 2 + 1) * D],
                                                        y_t[:, c, i * P:(i + 1) * P], w_v[:, c, :],
                                                        start=(c == 0), stop=(c == KC - 1))
                            if i % 2:
                                last.then_inc(m_full, 1)
                    project(t + AHEAD, (g + AHEAD) % GROUPS, m_use(b, 0, "yt1") if g else m_use(b, 0, "max") - 1)
                    if g == 1:
                        o_project(m_use(b, 1, "ot0"), m_use(b, 0, "o") + 2)
                    pe.wait_ge(stacked, (t + 1) * STACK_INC + STACK_INC)
                    for k in range(UNITS):
                        max_unit(t + 1, (g + 1) % GROUPS, k)
                        if k == 0:
                            pe.wait_ge(m_free, m_use(b, g, "max") + 2)
                            pe.wait_ge(x2_free, x2_max(t) + 2)
                        prob_unit(t, g, k)
                        if k == 3:
                            o_transposes(m_use(b, g, "o"), t + 1)
                        if k == 5:
                            if g == 0:
                                pe.wait_ge(m_free, m_use(b, 0, "v1") + 2)
                            pe.wait_ge(exps, t * UNITS + (2 + 4))
                            pe.wait_ge(pv_copied, t + 1)
                            pv(g, 0)
                        if k == 9:
                            pe.wait_ge(exps, t * UNITS + (2 + 8))
                            pv(g, 1)
                            pv(g, 3)
                    pe.wait_ge(exps, t * UNITS + (2 + UNITS))
                    pv(g, 2).then_inc(pv_done, 1)
                    if g == 0:
                        for c in range(KC):
                            y_transposes(m_use(b, 0, f"yt{c}"), b + 1, c)
            end = BATCH * M_PER + M_PRO
            o_transposes(end, STEPS + 1)
            o_project(end + 1, end + 2)

        @block.vector
        def _(dve):
            dve.sem_inc(maxes, 2)
            nc.vector.memset(v[:, :, :, HD:VW], 0.0).then_inc(init_done, 1)
            for g in range(GROUPS):
                nc.vector.memset(k_st[g][SROWS:P, :, :], 1.0).then_inc(v_const, 1)
            dve.wait_ge(init_done, 1)
            nc.vector.memset(v[:, :, :, HD:HD + 1], 1.0).then_inc(v_const, 1)
            nc.vector.memset(pv_sb[:, :], 1.0).then_inc(v_const, 1)
            nc.vector.memset(o_tok[:, :, :], 0.0).then_inc(v_const, 1)
            dve.sem_inc(x2_free, 1)
            if rope:
                dve.sem_inc(x1_free, 1)

            def normalise(b1, i):
                n = b1 * TPB + i
                nc.vector.tensor_scalar(y_tok[:, i, :], x[:, bass.ds(n, 1), :].rearrange("p a d -> p (a d)"),
                                        mean[:, bass.ds(n, 1)], rin[:, bass.ds(n, 1)], ALU.subtract,
                                        ALU.mult).then_inc(y_ready, 1)

            def rotate(t, g):
                if not isinstance(t, int) or t > 0:
                    dve.wait_ge(pool_chain, t * POOL_PER - (POOL_PER - 1))
                dve.wait_ge(x1_full, t + 1)
                nc.vector.scalar_tensor_tensor(part1[:, :], ps_x1[:, :], bias1[:, g:g + 1], rot1[:, :],
                                               ALU.add, ALU.mult).then_inc(x1_free, 1)
                dve.wait_ge(x2_full, x2_proj(t) + 1)
                nc.vector.scalar_tensor_tensor(part2[:, :], ps_x2[:, :], bias2[:, g:g + 1], rot2[:, :],
                                               ALU.add, ALU.mult).then_inc(x2_free, 1)

            def unit_max(t, k):
                dve.wait_ge(a_full, t * UNITS + (k + 1))
                ps = ps_a[k % 2]
                if k < 4:
                    work = [(nmax[:, 3, k:k + 1], ps[:, :])]
                elif k < 8:
                    work = [(nmax[:, 2, k - 4:k - 3], ps[:, 0:3 * P]), (nmax[:, 0, k - 4:k - 3], ps[:, 3 * P:SEQ])]
                else:
                    work = [(nmax[:, 1, 2 * (k - 8):2 * (k - 8) + 2], ps[:, :].rearrange("p (h n) -> p h n", h=2))]
                for out, src in work:
                    last = nc.vector.tensor_reduce(out, src, AX_X, ALU.max, negate=True)
                last.then_inc(maxes, 1)

            def rows_evac(t, slot):
                dve.wait_ge(x2_full, x2_max(t) + 1)
                nc.vector.tensor_copy(q_st[slot][SROWS:SROWS + PIECES, 2:4, :],
                                      ps_x2[:, :].bitcast(BF16)[SROWS:SROWS + PIECES, :].rearrange(
                                          "p (h s) -> p h s", h=2)).then_inc(x2_free, 1)

            def max_parts(t):
                dve.wait_ge(maxes, t * UNITS + (2 + UNITS))
                c = t * 3
                flat = lambda a: a[:, :, :].rearrange("p i h -> p (i h)")
                part = lambda r: nmax_p[:, :, :, r].rearrange("p i h -> p (i h)")
                nc.vector.tensor_copy(part(0), flat(nmax)).then_inc(dve_chain, 1)
                dve.wait_ge(dve_chain, c + 1)
                nc.vector.tensor_tensor(flat(nrest), flat(nmax), part(0), ALU.subtract).then_inc(dve_chain, 1)
                dve.wait_ge(dve_chain, c + 2)
                nc.vector.tensor_copy(part(1), flat(nrest)).then_inc(dve_chain, 1)
                dve.wait_ge(dve_chain, c + 3)
                nc.vector.tensor_tensor(part(2), flat(nrest), part(1), ALU.subtract).then_inc(nmax_ready, 1)

            def o_norm(use, g, n):
                dve.wait_ge(m_full, use + 1)
                ps = ps_m[:, :].rearrange("p (i h c) -> p i h c", h=HPG, c=VW)
                nc.vector.reciprocal(rsum[:, :, :], ps[:, :, :, HD]).then_inc(rsum_ready, 1)
                dve.wait_ge(rsum_ready, n)
                nc.vector.tensor_tensor(
                    o_tok[:, :, g * HPG * HD:(g + 1) * HPG * HD].rearrange("p i (h d) -> p i h d", d=HD),
                    ps[:, :, :, 0:HD],
                    rsum[:, :, :].unsqueeze(3).to_broadcast([P, TPB, HPG, HD]), ALU.mult).then_inc(m_free, 1)

            def out_evac(use, b0, half, rn):
                dve.wait_ge(m_full, use + 1)
                n = b0 * TPB + 2 * half
                dst = sub[:, bass.ds(n, 2), :]
                src = ps_m[:, :].rearrange("p (i d) -> p i d", i=2)
                if rope:
                    for i in range(2):
                        xn = x[:, bass.ds(n + i, 1), :].rearrange("p a d -> p (a d)")
                        nc.vector.tensor_scalar(resid[:, i, :], xn, mean[:, bass.ds(n + i, 1)],
                                                rstd[:, bass.ds(n + i, 1)], ALU.subtract, ALU.mult)\
                            .then_inc(out_chain, 1)
                    dve.wait_ge(out_chain, rn * 3 + 2)
                    nc.vector.tensor_tensor(resid[:, :, :], resid[:, :, :],
                                            bias_o[:, :].unsqueeze(1).to_broadcast([P, 2, D]), ALU.add)\
                        .then_inc(out_chain, 1)
                    dve.wait_ge(out_chain, rn * 3 + 3)
                    nc.vector.tensor_tensor(dst, src, resid[:, :, :], ALU.add).then_inc(m_free, 1)
                else:
                    nc.vector.tensor_copy(dst, src).then_inc(m_free, 1)

            for i in range(TPB):
                normalise(PADT // TPB, i)
            if rope:
                dve.wait_ge(weights_in, 16 * 11)
                for ahead in range(AHEAD):
                    rotate(ahead, ahead)
            for k in range(UNITS):
                unit_max(0, k)
            max_parts(0)
            with dve.Fori(0, BATCH) as b:
                for g in range(GROUPS):
                    t = b * GROUPS + g
                    rows_evac(t, g)
                    if g == 0 and rope:
                        for i in range(2):
                            dve.wait_ge(m_full, m_use(b, 0, f"v{i}") + 1)
                            nc.vector.tensor_tensor(v[:, 2 * i:2 * i + 2, :, 0:HD],
                                                    ps_m[:, :].rearrange("p (i h d) -> p i h d", i=2, d=HD),
                                                    bias_v[:, :].rearrange("p (h d) -> p h d", d=HD).unsqueeze(1)
                                                    .to_broadcast([P, 2, HEADS, HD]), ALU.add).then_inc(m_free, 1)
                    if rope:
                        rotate(t + AHEAD, (g + AHEAD) % GROUPS)
                    if g == 1:
                        for half in range(2):
                            out_evac(m_use(b, 1, f"out{half}"), b, half, b * 2 + half)
                    for k in range(UNITS):
                        unit_max(t + 1, k)
                        if g == 0 and k >= 5 and k < 5 + TPB:
                            normalise(b + 2, k - 5)
                        if k == 4:
                            o_norm(m_use(b, g, "o"), (g - 1) % GROUPS, t + 1)
                        if g == 1 and k >= 5 and k < 5 + TPB:
                            join.stats_of(sub, b * TPB, k - 5)
                        if g == 1 and k == 9:
                            join.sub_variance(dve, b)
                        if g == 2 and k >= 5 and k < 5 + TPB:
                            join.normalise_tile(dve, b, b * TPB, k - 5)
                        if g == 2 and k == 9:
                            join.add(dve, b, b * TPB)
                        if g == 3 and k < TPB:
                            join.stats_of(x, b * TPB, k)
                        if g == 3 and k == 5:
                            join.x_variance(dve, b, b * TPB)
                    max_parts(t + 1)
            end = BATCH * M_PER + M_PRO
            o_norm(end, GROUPS - 1, STEPS + 1)
            for half in range(2):
                out_evac(end + (3 + half), BATCH, half, 2 * BATCH + half)
            dve.wait_ge(m_free, end + 6)
            join.all_on_vector(dve, BATCH, BATCH * TPB)


def setup_phase(nc, keep, x_in, dispatched=None):
    x, ident, identb = keep["x"], keep["ident"], keep["identb"]
    with ExitStack() as ctx:
        filled, built = ctx.enter_context(nc.semaphore("filled")), ctx.enter_context(nc.semaphore("built"))
        zeroed = ctx.enter_context(nc.semaphore("zeroed"))
        block = ctx.enter_context(nc.Block())

        @block.sync
        def _(sp):
            for b in range(BATCH):
                sp.dma_start(x[:, PADT + b * TPB:PADT + (b + 1) * TPB, :],
                             x_in[b].rearrange("(n p) d -> p n d", p=P)).then_inc(keep["x_loaded"][b], 16)
            if dispatched is not None:
                sp.wait_ge(zeroed, 1)
                for e in range(E0 + 1):
                    sp.dma_start(dispatched[e * CAP:(e + 1) * CAP, :].rearrange("(p t) d -> p (t d)", t=CT),
                                 keep["zeros"][:, :]).then_inc(keep["cleared"], 16)

        @block.gpsimd
        def _(pool):
            nc.gpsimd.memset(keep["zeros"][:, :], 0.0).then_inc(zeroed, 1)
            fills = ((ident, 0.0), (identb, 0.0), (keep["mask_q"], 0.0), (keep["mask_k"], 0.0))
            for buf, value in fills:
                nc.gpsimd.memset(buf[:, :], value).then_inc(filled, 1)
            nc.gpsimd.memset(x[:, 0:PADT, :], 0.0).then_inc(built, 1)
            nc.gpsimd.memset(x[:, PADT + TILES:XT, :], 0.0).then_inc(built, 1)
            nc.gpsimd.memset(keep["sub"][:, 0:PADT, :], 0.0).then_inc(built, 1)
            pool.wait_ge(filled, len(fills))
            for m in (ident, identb):
                nc.gpsimd.affine_select(out=m[:, :], in_=m[:, :], compare_op=ALU.not_equal, fill=1.0, base=0,
                                        pattern=[[-1, P]], channel_multiplier=1).then_inc(built, 1)
            nc.gpsimd.affine_select(out=keep["mask_q"][:, :], in_=keep["mask_q"][:, :], compare_op=ALU.is_ge, fill=NEG,
                                    base=0, pattern=[[-1, P]], channel_multiplier=1).then_inc(built, 1)
            nc.gpsimd.affine_select(out=keep["mask_k"][:, :], in_=keep["mask_k"][:, :], compare_op=ALU.is_ge, fill=NEG,
                                    base=0, pattern=[[1, P]], channel_multiplier=-1).then_inc(built, 1)

        @block.vector
        def _(dve):
            for name, value in (("mean", 0.0), ("rstd", 1.0), ("rin", 1.0)):
                nc.vector.memset(keep[name][:, :], value)


def norm_phase(nc, keep):
    x, mean, rstd, rin = keep["x"], keep["mean"], keep["rstd"], keep["rin"]
    lo, hi = PADT, PADT + TILES
    with ExitStack() as ctx:
        def sb(n, shape, dt=F32):
            return ctx.enter_context(nc.sbuf_tensor(f"norm_{n}", shape, dt))

        def sem(n):
            return ctx.enter_context(nc.semaphore(f"norm_{n}"))

        stats = sb("stats", [P, TILES, 6])
        moments = sb("moments", [P, TILES, 2])
        var_eps, mean_sq = sb("var_eps", [P, TILES]), sb("mean_sq", [P, TILES])
        minus_half = sb("minus_half", [P, 1])
        chain, var_ready, root_ready, half_ready = sem("chain"), sem("var_ready"), sem("root_ready"), sem("half_ready")
        block = ctx.enter_context(nc.Block())

        @block.gpsimd
        def _(pool):
            nc.gpsimd.memset(minus_half[:, :], -0.5).then_inc(half_ready, 1)
            pool.wait_ge(half_ready, 1)
            for r, out in enumerate((rstd, rin)):
                pool.wait_ge(var_ready, r + 1)
                nc.gpsimd.tensor_tensor(out[:, lo:hi], var_eps[:, :], minus_half[:, :].to_broadcast([P, TILES]),
                                        ALU.pow).then_inc(root_ready, 1)

        @block.vector
        def _(dve):
            done = [0]

            def after(ins):
                done[0] += 1
                ins.then_inc(chain, 1)
                dve.wait_ge(chain, done[0])

            for n in range(TILES):
                if n % TPB == 0:
                    dve.wait_ge(keep["x_loaded"][n // TPB], 16)
                last = nc.vector.bn_stats(stats[:, n, :], x[:, lo + n, :])
            after(last)
            for n in range(TILES):
                last = nc.vector.bn_aggr(moments[:, n, :], stats[:, n, :])
            after(last)
            nc.vector.tensor_scalar(var_eps[:, :], moments[:, :, 1], EPS, None, ALU.add).then_inc(var_ready, 1)
            after(nc.vector.tensor_copy(mean[:, lo:hi], moments[:, :, 0]))
            dve.wait_ge(root_ready, 1)
            after(nc.vector.tensor_tensor(mean_sq[:, :], moments[:, :, 1], rstd[:, lo:hi], ALU.mult))
            after(nc.vector.tensor_tensor(mean_sq[:, :], mean_sq[:, :], rstd[:, lo:hi], ALU.mult))
            nc.vector.tensor_scalar(var_eps[:, :], mean_sq[:, :], EPS, None, ALU.add).then_inc(var_ready, 1)
            dve.wait_ge(root_ready, 2)
            after(nc.vector.tensor_tensor(rin[:, lo:hi], rin[:, lo:hi], rstd[:, lo:hi], ALU.mult))


def keep_all(nc, ctx):
    def sb(name, shape, dt=F32):
        return ctx.enter_context(nc.sbuf_tensor(f"kept_{name}", shape, dt))
    return {"x": sb("x", [P, XT, D]), "sub": sb("sub", [P, XT, D]), "mean": sb("mean", [P, XT]),
            "rstd": sb("rstd", [P, XT]), "rin": sb("rin", [P, XT]), "ident": sb("ident", [P, P]),
            "identb": sb("identb", [P, P], BF16), "mask_q": sb("mask_q", [P, P], BF16),
            "mask_k": sb("mask_k", [P, P], BF16), "zeros": sb("zeros", [P, CT * D])}


def rotation_tables():
    d = np.arange(P) // HPG % HD
    freqs = np.float32(10000.0) ** ((d % (HD // 2)).astype(np.float32) * np.float32(-2.0 / HD))
    ang = (np.arange(SEQ, dtype=np.float32)[None, :] * freqs[:, None].astype(np.float32)).astype(np.float32)
    even = (d % 2 == 0)[:, None]
    cos, sin = np.cos(ang), np.sin(ang)
    return (np.where(even, cos, sin).astype(np.float32), np.where(even, -sin, cos).astype(np.float32))


def stack_columns(wq, wk, order):
    def cols(a):
        heads = a.reshape(a.shape[0], GROUPS, HPG, HD)[..., order]
        return heads.transpose(0, 1, 3, 2).reshape(a.shape[0], GROUPS, HD * HPG)
    return np.concatenate([cols(wq), cols(wk)], axis=2)


def chunked(a):
    return np.ascontiguousarray(np.moveaxis(a.reshape(a.shape[0] // P, P, *a.shape[1:]), 0, 1))


def route_phase(nc, keep, w, route):
    x, sub, mean, rstd, ident = keep["x"], keep["sub"], keep["mean"], keep["rstd"], keep["ident"]
    with ExitStack() as ctx:
        def sb(n, shape, dt=F32):
            return ctx.enter_context(nc.sbuf_tensor(f"route_{n}", shape, dt))

        def psum(n, shape, dt=F32):
            return ctx.enter_context(nc.psum_tensor(f"route_{n}", shape, dt))

        def sem(n):
            return ctx.enter_context(nc.semaphore(f"route_{n}"))

        w_g = sb("w_g", [P, KC, E0])
        y_tok, y_t = sb("y_tok", [P, TPB, D]), sb("y_t", [P, KC, SEQ])
        logits, shifted, expd = sb("logits", [P, TILES, E0]), sb("shifted", [P, TILES, E0]), sb("expd", [P, TILES, E0])
        top, top_shift, top_exp = sb("top", [P, TILES, 8]), sb("top_shift", [P, TILES, 2]), sb("top_exp", [P, TILES, 2])
        top_at, top_atf = sb("top_at", [P, TILES, 8], U32), sb("top_atf", [P, TILES, 2])
        total, inv_total = sb("total", [P, TILES]), sb("inv_total", [P, TILES])
        numbers = sb("numbers", [P, E0])
        hot = sb("hot", [P, 2, TILES, E0])
        hot_sum = sb("hot_sum", [P, TILES, E0], BF16)
        before, ones = sb("before", [P, P], BF16), sb("ones", [P, P], BF16)
        ranks = sb("ranks", [P, TILES, E0])
        picked = sb("picked", [P, 2, TILES, E0])
        rank, kept, slot = sb("rank", [P, 2, TILES]), sb("kept", [P, 2, TILES]), sb("slot", [P, 2, TILES])
        far = sb("far", [P, 2, TILES])
        put_at = sb("put_at", [P, 2, TILES], U32)
        ps_t = [psum(f"ps_t{i}", [P, SEQ]) for i in range(2)]
        ps_l = psum("ps_l", [P, TPB, E0])
        ps_r = psum("ps_r", [P, TILES, E0])

        w_in, consts = sem("w_in"), sem("consts")
        y_ready, y_kept = sem("y_ready"), sem("y_kept")
        t_full, t_free, l_full, l_free = sem("t_full"), sem("t_free"), sem("l_full"), sem("l_free")
        chain, to_exp, exp_done = sem("chain"), sem("to_exp"), sem("exp_done")
        hot_ready, ranks_ready, slots_ready, scattered = (sem("hot_ready"), sem("ranks_ready"), sem("slots_ready"),
                                                          sem("scattered"))
        block = ctx.enter_context(nc.Block())

        @block.sync
        def _(sp):
            sp.dma_start(w_g[:, :, :], w["g"]).then_inc(w_in, 16)
            sp.wait_ge(w_in, 16)

        @block.gpsimd
        def _(pool):
            nc.gpsimd.iota(numbers[:, :], [[1, E0]], base=0, channel_multiplier=0,
                           allow_small_or_imprecise_dtypes=True).then_inc(consts, 1)
            nc.gpsimd.memset(ones[:, :], 1.0).then_inc(consts, 1)
            nc.gpsimd.memset(before[:, :], 1.0).then_inc(consts, 1)
            pool.wait_ge(consts, 3)
            nc.gpsimd.affine_select(out=before[:, :], in_=before[:, :], compare_op=ALU.is_gt, fill=0.0, base=0,
                                    pattern=[[1, P]], channel_multiplier=-1).then_inc(consts, 1)
            pool.wait_ge(slots_ready, 1)
            pool.wait_ge(keep["cleared"], 16 * (E0 + 1))
            pool.wait_ge(y_kept, TILES)
            for k in range(2):
                for n in range(TILES):
                    nc.gpsimd.indirect_dma_start(
                        out=w["dispatched"][:, :],
                        out_offset=bass.IndirectOffsetOnAxis(ap=put_at[:, k, n:n + 1], axis=0),
                        in_=sub[:, PADT + n, :], in_offset=None, bounds_check=SLOTS - 1,
                        oob_is_err=False).then_inc(scattered, 16)
            pool.wait_ge(scattered, 16 * 2 * TILES)

        @block.scalar
        def _(act):
            act.sem_inc(t_free, 2)
            with act.Fori(0, BATCH) as b:
                for c in range(KC):
                    act.wait_ge(t_full, b * KC + (c + 1))
                    nc.scalar.copy(y_t[:, c, :], ps_t[c][:, :]).then_inc(t_free, 1)
            act.wait_ge(to_exp, 2)
            nc.scalar.activation(expd[:, :, :], shifted[:, :, :], ACT.Exp).then_inc(exp_done, 1)
            nc.scalar.activation(top_exp[:, :, :], top_shift[:, :, :], ACT.Exp).then_inc(exp_done, 1)

        @block.tensor
        def _(pe):
            pe.sem_inc(l_free, 1)
            pe.wait_ge(w_in, 16)
            with pe.Fori(0, BATCH) as b:
                for c in range(KC):
                    pe.wait_ge(y_ready, b * TPB + TPB)
                    pe.wait_ge(t_free, b * KC + (c + 1))
                    for i in range(TPB):
                        last = nc.tensor.transpose(ps_t[c][:, i * P:(i + 1) * P], y_tok[:, i, c * P:(c + 1) * P],
                                                   ident[:, :])
                    last.then_inc(t_full, 1)
                pe.wait_ge(t_free, b * KC + (KC + 2))
                pe.wait_ge(l_free, b + 1)
                for i in range(TPB):
                    for c in range(KC):
                        last = nc.tensor.matmul(ps_l[:, i, :], y_t[:, c, i * P:(i + 1) * P], w_g[:, c, :],
                                                start=(c == 0), stop=(c == KC - 1))
                last.then_inc(l_full, 1)
            pe.wait_ge(consts, 4)
            pe.wait_ge(hot_ready, 1)
            for n in range(TILES):
                nc.tensor.matmul(ps_r[:, n, :], before[:, :], hot_sum[:, n, :], start=(n == 0), stop=True,
                                 skip_group_check=True)
            for n in range(TILES - 1):
                last = nc.tensor.matmul(ps_r[:, n + 1:TILES, :], ones[:, :],
                                        hot_sum[:, n:n + 1, :].to_broadcast([P, TILES - 1 - n, E0]),
                                        start=False, stop=True, skip_group_check=True)
            last.then_inc(ranks_ready, 1)

        @block.vector
        def _(dve):
            done = [0]

            def after(ins):
                done[0] += 1
                ins.then_inc(chain, 1)
                dve.wait_ge(chain, done[0])

            with dve.Fori(0, BATCH) as b:
                for i in range(TPB):
                    n = b * TPB + (PADT + i)
                    if i == 0:
                        dve.wait_ge(t_free, b * KC + 2)
                    xn = x[:, bass.ds(n, 1), :].rearrange("p a d -> p (a d)")
                    nc.vector.tensor_scalar(y_tok[:, i, :], xn, mean[:, bass.ds(n, 1)], rstd[:, bass.ds(n, 1)],
                                            ALU.subtract, ALU.mult).then_inc(y_ready, 1)
                    nc.vector.tensor_scalar(sub[:, bass.ds(n, 1), :].rearrange("p a d -> p (a d)"), xn,
                                            mean[:, bass.ds(n, 1)], rstd[:, bass.ds(n, 1)], ALU.subtract,
                                            ALU.mult).then_inc(y_kept, 1)
                dve.wait_ge(l_full, b + 1)
                nc.vector.tensor_copy(logits[:, bass.ds(b * TPB, TPB), :], ps_l[:, :, :]).then_inc(l_free, 1)
            dve.wait_ge(l_free, BATCH + 1)
            for n in range(TILES):
                last = nc.vector.max(top[:, n, :], logits[:, n, :])
            after(last)
            for n in range(TILES):
                last = nc.vector.max_index(top_at[:, n, :], top[:, n, :], logits[:, n, :])
            after(last)
            peak = top[:, :, 0:1]
            nc.vector.tensor_tensor(shifted[:, :, :], logits[:, :, :], peak.to_broadcast([P, TILES, E0]),
                                    ALU.subtract).then_inc(to_exp, 1)
            nc.vector.tensor_tensor(top_shift[:, :, :], top[:, :, 0:2], peak.to_broadcast([P, TILES, 2]),
                                    ALU.subtract).then_inc(to_exp, 1)
            after(nc.vector.tensor_copy(top_atf[:, :, :], top_at[:, :, 0:2]))
            dve.wait_ge(consts, 1)
            for k in range(2):
                after(nc.vector.tensor_tensor(hot[:, k, :, :], numbers[:, :].unsqueeze(1).to_broadcast([P, TILES, E0]),
                                              top_atf[:, :, k:k + 1].to_broadcast([P, TILES, E0]), ALU.is_equal))
            nc.vector.tensor_tensor(hot_sum[:, :, :], hot[:, 0, :, :], hot[:, 1, :, :], ALU.add).then_inc(hot_ready, 1)
            dve.wait_ge(exp_done, 2)
            after(nc.vector.tensor_reduce(total[:, :], expd[:, :, :], AX_X, ALU.add))
            after(nc.vector.reciprocal(inv_total[:, :], total[:, :]))
            gates = route["gates"]
            for k in range(2):
                after(nc.vector.tensor_tensor(gates[:, k, :], top_exp[:, :, k], inv_total[:, :], ALU.mult))
            dve.wait_ge(ranks_ready, 1)
            after(nc.vector.tensor_copy(ranks[:, :, :], ps_r[:, :, :]))
            for k in range(2):
                after(nc.vector.tensor_tensor(picked[:, k, :, :], hot[:, k, :, :], ranks[:, :, :], ALU.mult))
            after(nc.vector.tensor_reduce(rank[:, :, :], picked[:, :, :, :], AX_X, ALU.add))
            after(nc.vector.tensor_scalar(kept[:, :, :], rank[:, :, :], float(CAP), None, ALU.is_lt))
            for k in range(2):
                after(nc.vector.scalar_tensor_tensor(slot[:, k, :], top_atf[:, :, k], float(CAP), rank[:, k, :],
                                                     ALU.mult, ALU.add))
            after(nc.vector.tensor_scalar(far[:, :, :], kept[:, :, :], -2.0 * SLOTS, 2.0 * SLOTS, ALU.mult, ALU.add))
            after(nc.vector.tensor_tensor(far[:, :, :], far[:, :, :], slot[:, :, :], ALU.add))
            after(nc.vector.tensor_copy(put_at[:, :, :], far[:, :, :]))
            dve.sem_inc(slots_ready, 1)
            after(nc.vector.tensor_tensor(slot[:, :, :], slot[:, :, :], kept[:, :, :], ALU.mult))
            after(nc.vector.tensor_copy(route["get_at"][:, :, :], slot[:, :, :]))
            after(nc.vector.tensor_tensor(gates[:, :, :], gates[:, :, :], kept[:, :, :], ALU.mult))


def expert_phase(nc, keep, w):
    ident = keep["ident"]
    RING = 8
    TAKEN = ["u0", "v0", "u1", "u2", "u3", "u4", "v1", "u5", "u6", "u7", "t0", "t1", "t2", "o0", "o1", "o2"]
    DONE = ["u0", "u1", "u2", "u3", "v0", "u4", "u5", "u6", "u7", "v1", "t0", "t1", "t2", "o0", "o1", "o2"]
    BY_ACT = {"u0", "u2", "v0", "u4", "u6", "t0", "t2", "o1"}
    PAIR = 2
    taken = [(n, p) for p in range(PAIR) for n in TAKEN]
    finished = [(n, p) for p in range(PAIR) for n in DONE]
    T_FILLS = 3
    copies = {True: [f for f in finished if f[0] in BY_ACT], False: [f for f in finished if f[0] not in BY_ACT]}
    per = {who: len(v) for who, v in copies.items()}
    with ExitStack() as ctx:
        def sb(n, shape, dt=F32):
            return ctx.enter_context(nc.sbuf_tensor(f"exp_{n}", shape, dt))

        def sem(n):
            return ctx.enter_context(nc.semaphore(f"exp_{n}"))

        rows = [sb(f"rows{i}", [P, CT, D]) for i in range(PAIR)]
        w1 = [sb(f"w1_{i}", [P, KC, FF]) for i in range(PAIR)]
        w2 = [sb(f"w2_{i}", [P, FC, D]) for i in range(PAIR)]
        x_t = sb("x_t", [P, KC * CT * P])
        h = sb("h", [P, FC, CAP])
        out = [sb(f"out{i}", [P, CT * D]) for i in range(PAIR)]
        ps = [ctx.enter_context(nc.psum_tensor(f"exp_ps{i}", [P, SEQ], F32)) for i in range(RING)]

        rows_in, w1_in, w2_in, stored = [[sem(f"{n}{i}") for i in range(PAIR)]
                                         for n in ("rows_in", "w1_in", "w2_in", "stored")]
        full, first_t = sem("full"), sem("first_t")
        copied = {True: sem("copied_act"), False: sem("copied_dve")}
        gate = sem("gate")
        dispatched, results = w["dispatched"], w["results"]

        def full_at(it, name, p):
            return it * len(finished) + (T_FILLS + finished.index((name, p)) + 1)

        def copied_at(it, name, p, ago=0):
            who = name in BY_ACT
            return copied[who], it * per[who] + (per[who] * (1 - ago) + copies[who].index((name, p)) + 1)

        def bank(name, p):
            return ps[taken.index((name, p)) % RING]

        def dest(name):
            i = int(name[1])
            if name[0] == "u":
                return h[:, i, 0:SEQ], slice(0, SEQ), None
            if name[0] == "v":
                return h[:, 4 * i:4 * i + 4, SEQ:CAP], slice(0, SEQ), 4
            width = min(SEQ, KC * CAP - i * SEQ)
            return (lambda o: o[:, i * SEQ:i * SEQ + width]), slice(0, width), None

        def load(sp, what, e, p):
            if what == "rows":
                sp.dma_start(rows[p][:, :, :], dispatched[bass.ds(e * CAP, CAP), :].rearrange(
                    "(p t) d -> p t d", t=CT)).then_inc(rows_in[p], 16)
            elif what == "w1":
                sp.dma_start(w1[p][:, :, :], w["w1"][bass.ds(e, 1), :, :].rearrange(
                    "e (c p) f -> p (e c) f", p=P)).then_inc(w1_in[p], 16)
            else:
                sp.dma_start(w2[p][:, :, :], w["w2"][bass.ds(e, 1), :, :].rearrange(
                    "e (c p) d -> p (e c) d", p=P)).then_inc(w2_in[p], 16)

        def store(sp, it, p):
            for name in ("o1", "o2"):
                held(sp, gate, *copied_at(it, name, p))
            sp.dma_start(results[bass.ds((it * PAIR + p) * CAP, CAP), :].rearrange(
                "(p t) d -> p (t d)", t=CT), out[p][:, :]).then_inc(stored[p], 16)

        block = ctx.enter_context(nc.Block())

        @block.sync
        def _(sp):
            for p in range(PAIR):
                sp.sem_inc(stored[p], 16)
            load(sp, "rows", 0, 0)
            load(sp, "w1", 0, 0)
            load(sp, "rows", 1, 1)
            load(sp, "w2", 0, 0)
            load(sp, "w1", 1, 1)
            load(sp, "w2", 1, 1)
            sp.wait_ge(full, T_FILLS)
            load(sp, "rows", 2, 0)
            with sp.Fori(0, E0 // PAIR - 1) as it:
                for p in range(PAIR):
                    held(sp, gate, full, full_at(it, "v1", p))
                    load(sp, "w1", it * PAIR + (PAIR + p), p)
                    held(sp, gate, full, full_at(it, "t2", p))
                    load(sp, "rows", it * PAIR + (PAIR + p + 1), (p + 1) % PAIR)
                    held(sp, gate, full, full_at(it, "o2", p))
                    load(sp, "w2", it * PAIR + (PAIR + p), p)
                    store(sp, it, p)
            for p in range(PAIR):
                store(sp, E0 // PAIR - 1, p)
            for p in range(PAIR):
                sp.wait_ge(stored[p], 16 * (E0 // PAIR + 1))

        def copy_out(eng, it, who):
            for name, p in copies[who]:
                eng.wait_ge(full, full_at(it, name, p))
                to, cols, parts = dest(name)
                if name[0] == "t":
                    to = to(x_t)
                elif name[0] == "o":
                    if name in ("o0", "o1"):
                        eng.wait_ge(stored[p], it * 16 + 16)
                    to = to(out[p])
                src = bank(name, p)[:, cols]
                if parts:
                    src = src.rearrange("p (f n) -> p f n", f=parts)
                relu = name[0] in "uv"
                if who:
                    ins = nc.scalar.activation(to, src, ACT.Relu if relu else ACT.Copy)
                elif relu:
                    ins = nc.vector.tensor_scalar(to, src, 0.0, None, ALU.max)
                else:
                    ins = nc.vector.tensor_copy(to, src)
                ins.then_inc(copied[who], 1)

        def first_copies(eng, who):
            for i in range(T_FILLS):
                if (f"t{i}" in BY_ACT) == who:
                    eng.wait_ge(full, i + 1)
                    to, cols, _ = dest(f"t{i}")
                    src = bank(f"t{i}", 1)[:, cols]
                    (nc.scalar.copy if who else nc.vector.tensor_copy)(to(x_t), src).then_inc(first_t, 1)

        @block.scalar
        def _(act):
            act.sem_inc(copied[True], per[True])
            first_copies(act, True)
            with act.Fori(0, E0 // PAIR) as it:
                copy_out(act, it, True)

        @block.vector
        def _(dve):
            dve.sem_inc(copied[False], per[False])
            first_copies(dve, False)
            with dve.Fori(0, E0 // PAIR) as it:
                copy_out(dve, it, False)

        @block.tensor
        def _(pe):
            def take(it, name, p):
                c = taken.index((name, p)) - RING
                pe.wait_ge(*copied_at(it, *taken[c], ago=1 if c < 0 else 0))
                return bank(name, p)

            def transposes(it, p, banks):
                for n in range(KC * CT):
                    if n % 4 == 0:
                        out_ps = banks(n // 4)
                    c, t = divmod(n, CT)
                    last = nc.tensor.transpose(out_ps[:, n % 4 * P:(n % 4 + 1) * P],
                                               rows[(p + 1) % PAIR][:, t, c * P:(c + 1) * P], ident[:, :])
                    if n % 4 == 3 or n == KC * CT - 1:
                        last.then_inc(full, 1)

            def hidden(it, p):
                for f in range(FC):
                    u = take(it, f"u{f}", p)
                    if f % 4 == 0:
                        v = take(it, f"v{f // 4}", p)
                    at = (f % 4) * (CAP - SEQ)
                    for c in range(KC):
                        wt = w1[p][:, c, f * P:(f + 1) * P]
                        lu = nc.tensor.matmul(u[:, :], wt, x_t[:, c * CAP:c * CAP + SEQ], start=(c == 0),
                                              stop=(c == KC - 1))
                        lv = nc.tensor.matmul(v[:, at:at + CAP - SEQ], wt, x_t[:, c * CAP + SEQ:(c + 1) * CAP],
                                              start=(c == 0), stop=(c == KC - 1))
                    lu.then_inc(full, 1)
                    if f % 4 == 3:
                        lv.then_inc(full, 1)

            def outputs(it, p):
                for t in range(CT):
                    if t % 2 == 0:
                        o = take(it, f"o{t // 2}", p)
                    for f in range(FC):
                        last = nc.tensor.matmul(o[:, t % 2 * D:(t % 2 + 1) * D], h[:, f, t * P:(t + 1) * P],
                                                w2[p][:, f, :], start=(f == 0), stop=(f == FC - 1))
                    if t % 2 or t == CT - 1:
                        last.then_inc(full, 1)

            pe.wait_ge(rows_in[0], 16)
            transposes(None, 1, lambda i: bank(f"t{i}", 1))
            pe.wait_ge(first_t, T_FILLS)
            with pe.Fori(0, E0 // PAIR) as it:
                for p in range(PAIR):
                    for name in ("t1", "t2"):
                        pe.wait_ge(*copied_at(it, name, 1 - p, ago=1 - p))
                    pe.wait_ge(w1_in[p], it * 16 + 16)
                    hidden(it, p)
                    pe.wait_ge(rows_in[1 - p], it * 16 + 16 * (1 + p))
                    transposes(it, p, lambda i: take(it, f"t{i}", p))
                    for name in ("v0", "u6", "v1"):
                        pe.wait_ge(*copied_at(it, name, p))
                    pe.wait_ge(w2_in[p], it * 16 + 16)
                    outputs(it, p)


def combine_phase(nc, keep, w, route):
    x, sub, gates, get_at = keep["x"], keep["sub"], route["gates"], route["get_at"]
    DEEP = 6
    with ExitStack() as ctx:
        picked = [ctx.enter_context(nc.sbuf_tensor(f"comb_picked{i}", [P, 2, D], F32)) for i in range(DEEP)]
        scaled = ctx.enter_context(nc.sbuf_tensor("comb_scaled", [P, TILES, D], F32))
        gathered = [ctx.enter_context(nc.semaphore(f"comb_gathered{i}")) for i in range(DEEP)]
        scaled_done, summed = ctx.enter_context(nc.semaphore("comb_scaled_done")), ctx.enter_context(nc.semaphore("summed"))
        gate = ctx.enter_context(nc.semaphore("comb_gate"))
        join = Joining(nc, ctx, keep, "comb_join")
        block = ctx.enter_context(nc.Block())

        @block.gpsimd
        def _(pool):
            join.start_pool(pool)
            for b in range(BATCH + 2):
                for n in range(b * TPB, (b + 1) * TPB) if b < BATCH else ():
                    if n >= DEEP:
                        pool.wait_ge(summed, n - DEEP + 1)
                    for k in range(2):
                        nc.gpsimd.indirect_dma_start(
                            out=picked[n % DEEP][:, k, :], out_offset=None, in_=w["results"][:, :],
                            in_offset=bass.IndirectOffsetOnAxis(ap=get_at[:, k, n:n + 1], axis=0),
                            bounds_check=SLOTS - 1, oob_is_err=False).then_inc(gathered[n % DEEP], 16)
                if b >= 1 and b <= BATCH:
                    join.sub_root(pool, gate, b - 1)
                if b >= 2:
                    join.x_root(pool, gate, b - 2, PADT + (b - 2) * TPB)

        @block.vector
        def _(dve):
            for b in range(BATCH + 2):
                for i in range(TPB) if b < BATCH else ():
                    n = b * TPB + i
                    dve.wait_ge(gathered[n % DEEP], 32 * (n // DEEP + 1))
                    nc.vector.tensor_scalar(scaled[:, n, :], picked[n % DEEP][:, 0, :], gates[:, 0, n:n + 1], None,
                                            ALU.mult).then_inc(scaled_done, 1)
                    dve.wait_ge(scaled_done, n + 1)
                    nc.vector.scalar_tensor_tensor(sub[:, PADT + n, :], picked[n % DEEP][:, 1, :],
                                                   gates[:, 1, n:n + 1], scaled[:, n, :], ALU.mult,
                                                   ALU.add).then_inc(summed, 1)
                if b >= 1 and b <= BATCH:
                    n0 = PADT + (b - 1) * TPB
                    for i in range(TPB):
                        join.normalise_tile(dve, b - 1, n0, i)
                    join.add(dve, b - 1, n0)
                    for i in range(TPB):
                        join.stats_of(x, n0, i)
                    join.x_variance(dve, b - 1, n0)
                if b < BATCH:
                    dve.wait_ge(summed, (b + 1) * TPB)
                    for i in range(TPB):
                        join.stats_of(sub, PADT + b * TPB, i)
                    join.sub_variance(dve, b)


def dense_phase(nc, keep, w, out):
    x, sub, mean, rstd, ident = keep["x"], keep["sub"], keep["mean"], keep["rstd"], keep["ident"]
    NE = E1 + 1
    with ExitStack() as ctx:
        def sb(n, shape, dt=F32):
            return ctx.enter_context(nc.sbuf_tensor(f"dense_{n}", shape, dt))

        def psum(n, shape, dt=F32):
            return ctx.enter_context(nc.psum_tensor(f"dense_{n}", shape, dt))

        def sem(n):
            return ctx.enter_context(nc.semaphore(f"dense_{n}"))

        w_r = sb("w_r", [P, KC, NE])
        w_gate, w_up = sb("w_gate", [P, KC, HB * H1]), sb("w_up", [P, KC, HB * H1])
        w_down = sb("w_down", [P, HB, D])
        y_tok, y_t = sb("y_tok", [P, TPB, D]), sb("y_t", [P, KC, SEQ])
        scores = sb("scores", [P, TPB, NE])
        top, top_at, top_atf = sb("top", [P, TPB, 8]), sb("top_at", [P, TPB, 8], U32), sb("top_atf", [P, TPB, 2])
        diff, two = sb("diff", [P, 2, TPB]), sb("two", [P, 2, TPB])
        numbers = sb("numbers", [P, E1])
        hot, mix = sb("hot", [P, 2, TPB, E1]), sb("mix", [P, TPB, NE])
        gated = [sb(f"gated{i}", [P, SEQ]) for i in range(2)]
        h = sb("h", [P, HB, SEQ])
        ps_t = [psum(f"ps_t{i}", [P, SEQ]) for i in range(KC)]
        ps_g = [psum(f"ps_g{i}", [P, SEQ]) for i in range(2)]
        ps_u = [psum(f"ps_u{i}", [P, SEQ]) for i in range(2)]
        ps_d = [psum(f"ps_d{i}", [P, SEQ]) for i in range(2)]

        w_in, wide_in, consts = sem("w_in"), sem("wide_in"), sem("consts")
        y_ready, t_full, t_free = sem("y_ready"), sem("t_full"), sem("t_free")
        s_full, s_free = sem("s_full"), sem("s_free")
        g_full, silu_done, u_full, h_done = sem("g_full"), sem("silu_done"), sem("u_full"), sem("h_done")
        d_full, d_free = sem("d_full"), sem("d_free")
        chain, diff_ready, two_ready, gate = sem("chain"), sem("diff_ready"), sem("two_ready"), sem("gate")
        stored = sem("stored")
        join = Joining(nc, ctx, keep, "dense_join", then_stats=False)
        block = ctx.enter_context(nc.Block())
        D_FILLS = (NE + 1) // 2

        @block.sync
        def _(sp):
            sp.dma_start(w_r[:, :, :], w["r"]).then_inc(w_in, 16)
            sp.dma_start(w_gate[:, :, :], w["gate"]).then_inc(wide_in, 16)
            sp.dma_start(w_up[:, :, :], w["up"]).then_inc(wide_in, 16)
            sp.dma_start(w_down[:, :, :], w["down"]).then_inc(wide_in, 16)
            sp.wait_ge(w_in, 16)
            sp.wait_ge(wide_in, 48)
            for b in range(BATCH):
                held(sp, gate, join.joined, b + 2)
                sp.dma_start(out[b].rearrange("(n p) d -> p n d", p=P),
                             x[:, PADT + b * TPB:PADT + (b + 1) * TPB, :]).then_inc(stored, 16)
            sp.wait_ge(stored, 16 * BATCH)

        @block.gpsimd
        def _(pool):
            nc.gpsimd.iota(numbers[:, :], [[1, E1]], base=0, channel_multiplier=0,
                           allow_small_or_imprecise_dtypes=True).then_inc(consts, 1)
            join.start_pool(pool)
            with pool.Fori(0, BATCH + 1) as b:
                join.sub_root(pool, gate, b)

        @block.scalar
        def _(act):
            act.sem_inc(t_free, KC)
            act.sem_inc(silu_done, 2)
            with act.Fori(0, BATCH) as b:
                for c in range(KC):
                    act.wait_ge(t_full, b * KC + (c + 1))
                    nc.scalar.copy(y_t[:, c, :], ps_t[c][:, :]).then_inc(t_free, 1)
                for n in range(HB):
                    act.wait_ge(g_full, b * HB + (n + 1))
                    act.wait_ge(h_done, b * HB + (n + 1))
                    nc.scalar.activation(gated[n % 2][:, :], ps_g[n % 2][:, :], ACT.Silu).then_inc(silu_done, 1)
                    if n == 3:
                        act.wait_ge(diff_ready, b + 1)
                        nc.scalar.activation(two[:, :, :], diff[:, :, :], ACT.Sigmoid).then_inc(two_ready, 1)
                        nc.scalar.activation(mix[:, :, E1], scores[:, :, E1], ACT.Sigmoid).then_inc(two_ready, 1)

        @block.tensor
        def _(pe):
            pe.sem_inc(s_free, 1)
            pe.wait_ge(w_in, 16)
            pe.wait_ge(wide_in, 48)
            with pe.Fori(0, BATCH) as b:
                for c in range(KC):
                    pe.wait_ge(y_ready, b * TPB + TPB)
                    pe.wait_ge(t_free, b * KC + (c + 1))
                    if c == 0:
                        pe.wait_ge(s_free, b + 1)
                    for i in range(TPB):
                        last = nc.tensor.transpose(ps_t[c][:, i * P:(i + 1) * P], y_tok[:, i, c * P:(c + 1) * P],
                                                   ident[:, :])
                    last.then_inc(t_full, 1)
                pe.wait_ge(t_free, b * KC + 2 * KC)
                for i in range(TPB):
                    for c in range(KC):
                        last = nc.tensor.matmul(ps_t[0][:, i * NE:(i + 1) * NE], y_t[:, c, i * P:(i + 1) * P],
                                                w_r[:, c, :], start=(c == 0), stop=(c == KC - 1))
                last.then_inc(s_full, 1)
                for n in range(HB):
                    pe.wait_ge(silu_done, b * HB + (n + 1))
                    for c in range(KC):
                        last = nc.tensor.matmul(ps_g[n % 2][:, :], w_gate[:, c, n * H1:(n + 1) * H1], y_t[:, c, :],
                                                start=(c == 0), stop=(c == KC - 1))
                    last.then_inc(g_full, 1)
                    pe.wait_ge(h_done, b * HB + (n + 1))
                    for c in range(KC):
                        last = nc.tensor.matmul(ps_u[n % 2][:, :], w_up[:, c, n * H1:(n + 1) * H1], y_t[:, c, :],
                                                start=(c == 0), stop=(c == KC - 1))
                    last.then_inc(u_full, 1)
                for i in range(TPB):
                    for e in range(NE):
                        at = e % 2 * D
                        if e % 2 == 0:
                            pe.wait_ge(d_free, (b * TPB + i) * D_FILLS + (e // 2 + 1))
                            pe.wait_ge(h_done, b * HB + (2 + min(HB, e + 2)))
                            o = ps_d[(i * D_FILLS + e // 2) % 2]
                        blocks = [e] if e < E1 else [E1, E1 + 1]
                        if e == E1:
                            pe.wait_ge(h_done, b * HB + (2 + HB))
                        for n in blocks:
                            last = nc.tensor.matmul(o[:, at:at + D], h[:, n, i * P:(i + 1) * P], w_down[:, n, :],
                                                    start=(n == blocks[0]), stop=(n == blocks[-1]))
                        if e % 2 or e == NE - 1:
                            last.then_inc(d_full, 1)

        @block.vector
        def _(dve):
            dve.sem_inc(h_done, 2)
            dve.sem_inc(d_free, 2)

            def after(ins, b, c):
                ins.then_inc(chain, 1)
                dve.wait_ge(chain, b * CHAIN_N + c)

            CHAIN_N = 7 + TPB * NE
            def normalise(b, i):
                n = b * TPB + (PADT + i)
                xn = x[:, bass.ds(n, 1), :].rearrange("p a d -> p (a d)")
                nc.vector.tensor_scalar(y_tok[:, i, :], xn, mean[:, bass.ds(n, 1)], rstd[:, bass.ds(n, 1)],
                                        ALU.subtract, ALU.mult).then_inc(y_ready, 1)

            dve.wait_ge(consts, 1)
            for i in range(TPB):
                normalise(0, i)
            with dve.Fori(0, BATCH) as b:
                dve.wait_ge(s_full, b + 1)
                nc.vector.tensor_copy(scores[:, :, :], ps_t[0][:, 0:TPB * NE].rearrange("p (i e) -> p i e", e=NE))                    .then_inc(s_free, 1)
                held(dve, gate, s_free, b + 2)
                for i in range(TPB):
                    last = nc.vector.max(top[:, i, :], scores[:, i, 0:E1])
                last.then_inc(chain, 1)
                held(dve, gate, chain, b * CHAIN_N + 1)
                for i in range(TPB):
                    last = nc.vector.max_index(top_at[:, i, :], top[:, i, :], scores[:, i, 0:E1])
                after(last, b, 2)
                after(nc.vector.tensor_tensor(diff[:, 0, :], top[:, :, 0], top[:, :, 1], ALU.subtract), b, 3)
                nc.vector.tensor_scalar(diff[:, 1, :], diff[:, 0, :], -1.0, None, ALU.mult).then_inc(diff_ready, 1)
                after(nc.vector.tensor_copy(top_atf[:, :, :], top_at[:, :, 0:2]), b, 4)
                for k in range(2):
                    last = nc.vector.tensor_tensor(hot[:, k, :, :], numbers[:, :].unsqueeze(1).to_broadcast([P, TPB, E1]),
                                                   top_atf[:, :, k:k + 1].to_broadcast([P, TPB, E1]), ALU.is_equal)
                after(last, b, 5)
                for n in range(HB):
                    dve.wait_ge(silu_done, b * HB + (2 + n + 1))
                    dve.wait_ge(u_full, b * HB + (n + 1))
                    nc.vector.tensor_tensor(h[:, n, :], gated[n % 2][:, :], ps_u[n % 2][:, :],
                                            ALU.mult).then_inc(h_done, 1)
                    if n < TPB:
                        join.stats_of(sub, b * TPB, n)
                    if n == TPB:
                        join.sub_variance(dve, b)
                    if n == 7:
                        for i in range(TPB):
                            join.normalise_tile(dve, b, b * TPB, i)
                        join.add(dve, b, b * TPB)
                    if n == 6:
                        dve.wait_ge(two_ready, b * 2 + 2)
                        for k in range(2):
                            last = nc.vector.tensor_tensor(hot[:, k, :, :], hot[:, k, :, :],
                                                           two[:, k, :].unsqueeze(2).to_broadcast([P, TPB, E1]), ALU.mult)
                        after(last, b, 6)
                        after(nc.vector.tensor_tensor(mix[:, :, 0:E1], hot[:, 0, :, :], hot[:, 1, :, :], ALU.add), b, 7)
                for i in range(TPB):
                    acc = sub[:, bass.ds(b * TPB + (PADT + i), 1), :].rearrange("p a d -> p (a d)")
                    for e in range(NE):
                        o = ps_d[(i * D_FILLS + e // 2) % 2][:, e % 2 * D:(e % 2 + 1) * D]
                        if e % 2 == 0:
                            dve.wait_ge(d_full, (b * TPB + i) * D_FILLS + (e // 2 + 1))
                        if e == 0:
                            ins = nc.vector.tensor_scalar(acc, o, mix[:, i, e:e + 1], None, ALU.mult)
                        else:
                            dve.wait_ge(chain, b * CHAIN_N + (7 + i * NE + e))
                            ins = nc.vector.scalar_tensor_tensor(acc, o, mix[:, i, e:e + 1], acc, ALU.mult, ALU.add)
                        ins.then_inc(chain, 1)
                        if e % 2 or e == NE - 1:
                            dve.wait_ge(chain, b * CHAIN_N + (7 + i * NE + e + 1))
                            dve.sem_inc(d_free, 1)
                    normalise(b + 1, i)
            join.all_on_vector(dve, BATCH, BATCH * TPB)


def program(nc, io, out):
    with ExitStack() as ctx:
        keep = keep_all(nc, ctx)
        scratch = nc.dram_tensor("scratch", (2, 2, len(Q_STACK), HD, HPG, SEQ), BF16, kind="Internal").ap()
        dispatched = nc.dram_tensor("dispatched", ((E0 + 1) * CAP, D), F32, kind="Internal").ap()
        results = nc.dram_tensor("results", (SLOTS, D), F32, kind="Internal").ap()
        keep["cleared"] = ctx.enter_context(nc.semaphore("cleared"))
        keep["x_loaded"] = [ctx.enter_context(nc.semaphore(f"x_loaded{b}")) for b in range(BATCH)]
        setup_phase(nc, keep, io["x"], dispatched)
        norm_phase(nc, keep)
        attention_phase(nc, keep, {n[3:]: a for n, a in io.items() if n.startswith("a0_")} | {"scratch": scratch}, 0)
        with ExitStack() as moe:
            route = {"gates": moe.enter_context(nc.sbuf_tensor("gates", [P, 2, TILES], F32)),
                     "get_at": moe.enter_context(nc.sbuf_tensor("get_at", [P, 2, TILES], U32))}
            w = {n[3:]: a for n, a in io.items() if n.startswith("m0_")} | {"dispatched": dispatched, "results": results}
            route_phase(nc, keep, w, route)
            expert_phase(nc, keep, w)
            combine_phase(nc, keep, w, route)
        attention_phase(nc, keep, {n[3:]: a for n, a in io.items() if n.startswith("a1_")} | {"scratch": scratch}, 1)
        dense_phase(nc, keep, {n[3:]: a for n, a in io.items() if n.startswith("m1_")}, out)


def laid_out(inputs):
    a = {n: np.asarray(v) for n, v in inputs.items()}
    even = [2 * (d % (HD // 2)) for d in range(HD)]
    odd = [2 * (d % (HD // 2)) + 1 for d in range(HD)]
    same = list(range(HD))
    g = {n[len("L0_attn_"):]: v for n, v in a.items() if n.startswith("L0_attn_")}
    r = {"x": g["x"]}
    r["a0_x1"] = chunked(stack_columns(g["wq"], g["wk"], even))
    r["a0_x2"] = chunked(stack_columns(g["wq"], g["wk"], odd))
    r["a0_v"], r["a0_o"] = chunked(g["wv"]), chunked(g["wo"])
    r["a0_bias1"] = stack_columns(g["bq"][None], g["bk"][None], even)[0].T
    r["a0_bias2"] = stack_columns(g["bq"][None], g["bk"][None], odd)[0].T
    r["a0_bias_v"], r["a0_bias_o"] = np.tile(g["bv"][None], (P, 1)), np.tile(g["bo"][None], (P, 1))
    r["a0_rms_w"] = chunked(g["rms_w"])
    r["a0_rot1"], r["a0_rot2"] = rotation_tables()
    r["m0_g"] = chunked(a["L0_ffn_Wg"])
    r["m0_w1"], r["m0_w2"] = a["L0_ffn_w1"], a["L0_ffn_w2"]
    qkv = a["L1_attn_W_qkv"].T
    r["a1_x1"] = chunked(stack_columns(qkv[:, 0:D], qkv[:, D:2 * D], same))
    r["a1_v"], r["a1_o"] = chunked(qkv[:, 2 * D:3 * D]), chunked(a["L1_attn_W_proj"].T)
    f = {n[len("L1_ffn_"):]: v for n, v in a.items() if n.startswith("L1_ffn_")}
    r["m1_r"] = chunked(np.concatenate([f["gate_w"], f["se_gate_w"]]).T)
    for n in ("gate", "up"):
        r[f"m1_{n}"] = chunked(np.concatenate([f[f"w_{n}"].reshape(E1 * H1, D), f[f"sh_{n}"]]).T)
    down = np.concatenate([f["w_down"].transpose(0, 2, 1).reshape(E1 * H1, D), f["sh_down"].T])
    r["m1_down"] = chunked(down)
    return {n: np.ascontiguousarray(v) for n, v in r.items()}


def kernel(**inputs):
    import concourse.bacc as bacc
    from concourse.bass_utils import run_bass_kernel_spmd

    nc = bacc.Bacc("TRN2", target_bir_lowering=False, num_devices=1)
    arrays = {f"in_{n}": v for n, v in laid_out(inputs).items()}
    io = {n[3:]: nc.dram_tensor(n, v.shape, mybir.dt.from_np(v.dtype), kind="ExternalInput").ap()
          for n, v in arrays.items()}
    out = nc.dram_tensor("out", (BATCH, SEQ, D), F32, kind="ExternalOutput").ap()
    program(nc, io, out)
    return run_bass_kernel_spmd(nc, [arrays], core_ids=[0]).results[0]["out"]
```

```python
from contextlib import ExitStack

import numpy as np

import concourse.bass as bass
from concourse import mybir

F32 = mybir.dt.float32
BF16 = mybir.dt.bfloat16
F32R = mybir.dt.float32r
I32 = mybir.dt.int32
U32 = mybir.dt.uint32
ALU = mybir.AluOpType
ACT = mybir.ActivationFunctionType
AX_X = mybir.AxisListType.X

P = 128
BATCH, SEQ, D = 4, 512, 256
HEADS, HD = 16, 16
KC = D // P
TPB = SEQ // P
TILES = BATCH * TPB
PADT = TPB
XT = TILES + 2 * PADT
GROUPS = 4
HPG = HEADS // GROUPS
STEPS = BATCH * GROUPS
EPS = 1e-5
NEG = -1e38
PIECES = 3
Q_STACK = (0, 0, 0, 1, 1, 2)
K_STACK = (0, 1, 2, 0, 1, 0)
SROWS = len(Q_STACK) * HD
VW = 32
UNITS = 10

E0, FF, CAP = 8, 1024, 640
FC = FF // P
CT = CAP // P
SLOTS = E0 * CAP
E1, H1 = 8, 128
HB = E1 + 2


def held(eng, gate, on, value):
    eng.wait_ge(on, value)
    eng.sem_inc(gate, 1)


class Joining:

    def __init__(self, nc, ctx, keep, tag, then_stats=True):
        self.nc, self.keep, self.then_stats = nc, keep, then_stats
        sb = lambda n, shape: ctx.enter_context(nc.sbuf_tensor(f"{tag}_{n}", shape, F32))
        sem = lambda n: ctx.enter_context(nc.semaphore(f"{tag}_{n}"))
        self.stats, self.moments = sb("stats", [P, TPB, 6]), sb("moments", [P, 2, TPB, 2])
        self.var_eps, self.inv = sb("var_eps", [P, 2, TPB]), sb("inv", [P, TPB])
        self.norm_chain, self.var_ready, self.root_ready, self.joined = (
            sem("norm_chain"), sem("var_ready"), sem("root_ready"), sem("joined"))
        self.gate, self.minus_half = keep["gate"], keep["minus_half"]
        self.CHAIN = 7 if then_stats else 4
        self.VARS = 2 if then_stats else 1

    def stats_of(self, src, n0, i):
        ins = self.nc.vector.bn_stats(self.stats[:, i, :],
                                      src[:, bass.ds(n0 + i, 1), :].rearrange("p a d -> p (a d)"))
        if i == TPB - 1:
            ins.then_inc(self.norm_chain, 1)

    def variance(self, dve, which, k, c):
        nc = self.nc
        held(dve, self.gate, self.norm_chain, k * self.CHAIN + c)
        for i in range(TPB):
            last = nc.vector.bn_aggr(self.moments[:, which, i, :], self.stats[:, i, :])
        last.then_inc(self.norm_chain, 1)
        dve.wait_ge(self.norm_chain, k * self.CHAIN + (c + 1))
        nc.vector.tensor_scalar(self.var_eps[:, which, :], self.moments[:, which, :, 1], EPS, None,
                                ALU.add).then_inc(self.var_ready, 1)

    def sub_variance(self, dve, k):
        self.variance(dve, 0, k, 1)

    def normalise_tile(self, dve, k, n0, i):
        sub = self.keep["sub"]
        tile = sub[:, bass.ds(n0 + i, 1), :].rearrange("p a d -> p (a d)")
        if i == 0:
            dve.wait_ge(self.root_ready, k * self.VARS + 1)
        ins = self.nc.vector.tensor_scalar(tile, tile, self.moments[:, 0, i, 0:1], self.inv[:, i:i + 1],
                                           ALU.subtract, ALU.mult)
        if i == TPB - 1:
            ins.then_inc(self.norm_chain, 1)

    def add(self, dve, k, n0):
        x, sub = self.keep["x"], self.keep["sub"]
        dve.wait_ge(self.norm_chain, k * self.CHAIN + 3)
        self.nc.vector.tensor_tensor(x[:, bass.ds(n0, TPB), :], x[:, bass.ds(n0, TPB), :],
                                     sub[:, bass.ds(n0, TPB), :], ALU.add).then_inc(self.norm_chain, 1)
        dve.wait_ge(self.norm_chain, k * self.CHAIN + 4)
        dve.sem_inc(self.joined, 1)

    def x_variance(self, dve, k, n0):
        self.variance(dve, 1, k, 5)
        self.nc.vector.tensor_copy(self.keep["mean"][:, bass.ds(n0, TPB)],
                                   self.moments[:, 1, :, 0]).then_inc(self.norm_chain, 1)

    def all_on_vector(self, dve, k, n0):
        for i in range(TPB):
            self.stats_of(self.keep["sub"], n0, i)
        self.sub_variance(dve, k)
        for i in range(TPB):
            self.normalise_tile(dve, k, n0, i)
        self.add(dve, k, n0)
        if self.then_stats:
            for i in range(TPB):
                self.stats_of(self.keep["x"], n0, i)
            self.x_variance(dve, k, n0)

    def sub_root(self, pool, gate, k):
        held(pool, gate, self.var_ready, k * self.VARS + 1)
        self.nc.gpsimd.tensor_tensor(self.inv[:, :], self.var_eps[:, 0, :],
                                     self.minus_half[:, :].to_broadcast([P, TPB]), ALU.pow)\
            .then_inc(self.root_ready, 1)

    def x_root(self, pool, gate, k, n0):
        held(pool, gate, self.var_ready, k * 2 + 2)
        for name in ("rstd", "rin"):
            last = self.nc.gpsimd.tensor_tensor(self.keep[name][:, bass.ds(n0, TPB)], self.var_eps[:, 1, :],
                                                self.minus_half[:, :].to_broadcast([P, TPB]), ALU.pow)
        last.then_inc(self.root_ready, 1)


PASSES = ((0, 0), (0, 1), (1, 0))


def attention_phase(nc, keep, w, layer, wide=None):
    wide = wide or []
    rope = layer == 0
    scale = float(HD) ** -0.5 if rope else float(D) ** -0.5
    x, sub, mean, rstd, rin = keep["x"], keep["sub"], keep["mean"], keep["rstd"], keep["rin"]
    ident, identb, mask_q, mask_k = keep["ident"], keep["identb"], keep["mask_q"], keep["mask_k"]
    RUNS = (((0, 3, 0, 0), (3, 2, 1, 0), (5, 1, 2, 0)), ((0, 3, 0, 1), (3, 2, 0, 1), (5, 1, 0, 0)))
    OUT_INC, STACK_INC = 16 * 6, 16 * 2
    with ExitStack() as ctx:
        def sb(name, shape, dt=F32):
            return ctx.enter_context(nc.sbuf_tensor(f"a{layer}_{name}", shape, dt))

        def psum(name, shape, dt=F32):
            return ctx.enter_context(nc.psum_tensor(f"a{layer}_{name}", shape, dt))

        def sem(name):
            return ctx.enter_context(nc.semaphore(f"a{layer}_{name}"))

        w_x1 = sb("w_x1", [P, KC, GROUPS, P])
        w_v = sb("w_v", [P, KC, D])
        w_o = sb("w_o", [P, KC, D])
        if rope:
            w_x2 = sb("w_x2", [P, KC, GROUPS, P])
            bias1, bias2 = sb("bias1", [P, GROUPS]), sb("bias2", [P, GROUPS])
            bias_v, bias_o = sb("bias_v", [P, D]), sb("bias_o", [P, D])
            rms_w = sb("rms_w", [P, KC])
            rot1, rot2 = sb("rot1", [P, SEQ]), sb("rot2", [P, SEQ])
            part2 = sb("part2", [P, SEQ])
            resid = sb("resid", [P, 2, D])
        part1 = sb("part1", [P, SEQ])
        y_tok = sb("y_tok", [P, TPB, D])
        y_t = sb("y_t", [P, KC, SEQ])
        qk = sb("qk", [P, SEQ]) if rope else part1
        rest1 = sb("rest1", [P, SEQ])
        pieces = sb("pieces", [P, PIECES, SEQ], BF16)
        q_st = [sb(f"q_st{g}", [P, HPG, SEQ], BF16) for g in range(GROUPS)]
        k_st = [sb(f"k_st{g}", [P, HPG, SEQ], BF16) for g in range(GROUPS)]
        v = sb("v", [P, TPB, HEADS, VW])
        probs = sb("probs", [P, UNITS, SEQ])
        nmax = sb("nmax", [P, TPB, HPG])
        nrest = sb("nrest", [P, TPB, HPG])
        nmax_p = sb("nmax_p", [P, TPB, HPG, PIECES], BF16)
        pv_sb = sb("pv_sb", [P, SEQ])
        rsum = sb("rsum", [P, TPB, HPG])
        o_tok = sb("o_tok", [P, TPB, D])
        o_t = sb("o_t", [P, KC, SEQ])

        ps_a = [psum(f"ps_a{i}", [P, SEQ]) for i in range(2)]
        ps_b = [psum(f"ps_b{i}", [P, SEQ]) for i in range(2)]
        ps_pv = psum("ps_pv", [P, SEQ])
        ps_x1 = psum("ps_x1", [P, SEQ])
        ps_x2 = psum("ps_x2", [P, SEQ])
        ps_m = psum("ps_m", [P, SEQ])

        weights_in = sem("weights_in")
        v_const = sem("v_const")
        y_ready = sem("y_ready")
        x1_full, x1_free = sem("x1_full"), sem("x1_free")
        x2_full, x2_free = sem("x2_full"), sem("x2_free")
        m_full, m_free = sem("m_full"), sem("m_free")
        pool_chain = sem("pool_chain")
        dve_chain = sem("dve_chain")
        pieces_out = sem("pieces_out")
        stacked = sem("stacked")
        a_full, maxes = sem("a_full"), sem("maxes")
        b_full, exps = sem("b_full"), sem("exps")
        nmax_ready, copies = sem("nmax_ready"), sem("copies")
        pv_done, pv_copied = sem("pv_done"), sem("pv_copied")
        rsum_ready = sem("rsum_ready")
        out_chain = sem("out_chain")
        init_done = sem("init_done")

        scratch = w["scratch"]

        AHEAD = 3
        M_PRO, M_PER = KC, 16
        M_AT = {}
        n = 0
        for g in range(GROUPS):
            uses = ["max"]
            if g == 0:
                uses += ["v0", "v1"]
            if g == 1:
                uses += ["ot0", "ot1", "out0", "out1"]
            uses += ["o"]
            if g == 0:
                uses += ["yt0", "yt1"]
            for u in uses:
                M_AT[(g, u)] = n
                n += 1
        assert n == M_PER

        def m_use(b, g, u):
            return b * M_PER + (M_PRO + M_AT[(g, u)])

        def x2_proj(t):
            return t if isinstance(t, int) else t * 2 - (AHEAD - 1)

        def x2_max(t):
            return t * 2 + AHEAD if rope else t

        POOL_PER = 3 if rope else 2

        gate = keep["gate"]
        wide_in, wide_hi, wide_lo = sem("wide_in"), sem("wide_hi"), sem("wide_lo")
        join = Joining(nc, ctx, keep, f"a{layer}_join")

        SHARE = wide[0][1].shape[-1] // BATCH if wide else 1
        wide_raw = [sb(f"wide_raw{n}", [P, KC, SHARE]) for n in range(len(wide))]

        def wide_cols(a, b):
            return a[:, :, bass.ds(b * SHARE, SHARE)]

        block = ctx.enter_context(nc.Block())

        @block.sync
        def _(sp):
            loads = [(w_x1[:, :, :, :], w["x1"]), (w_v[:, :, :], w["v"]), (w_o[:, :, :], w["o"])]
            if rope:
                loads += [(w_x2[:, :, :, :], w["x2"]), (bias1[:, :], w["bias1"]), (bias2[:, :], w["bias2"]),
                          (bias_v[:, :], w["bias_v"]), (bias_o[:, :], w["bias_o"]), (rms_w[:, :], w["rms_w"]),
                          (rot1[:, :], w["rot1"]), (rot2[:, :], w["rot2"])]
            for dst, src in loads:
                sp.dma_start(dst, src).then_inc(weights_in, 16)

            def restack(b, g, ahead):
                t = b * GROUPS + (g + ahead)
                slot = (g + ahead) % GROUPS
                held(sp, gate, pool_chain, t * POOL_PER + POOL_PER)
                for half, runs in enumerate(RUNS):
                    rows = slice(half * HPG * HD, (half + 1) * HPG * HD)
                    for r, n, i, step in runs:
                        src = pieces[rows, i:i + n, :] if step else pieces[rows, i:i + 1, :].to_broadcast(
                            [HPG * HD, n, SEQ])
                        sp.dma_start(scratch[slot % 2, half, r:r + n].rearrange("r d h s -> (d h) r s"), src)\
                          .then_inc(pieces_out, 16)
                held(sp, gate, pieces_out, t * OUT_INC + OUT_INC)
                if ahead == AHEAD:
                    held(sp, gate, pv_done, b * GROUPS + (g + 2))
                for half, st in enumerate((q_st[slot], k_st[slot])):
                    sp.dma_start(st[0:SROWS, :, :], scratch[slot % 2, half].rearrange("r d h s -> (r d) h s"))\
                      .then_inc(stacked, 16)
                held(sp, gate, stacked, t * STACK_INC + STACK_INC)

            for ahead in range(AHEAD):
                restack(0, 0, ahead)
            with sp.Fori(0, BATCH) as b:
                for g in range(GROUPS):
                    restack(b, g, AHEAD)
                    if g == 0 and wide:
                        held(sp, gate, wide_lo, b * len(wide) + 1)
                        for n, (src, _, _) in enumerate(wide):
                            sp.dma_start(wide_raw[n][:, :, :], wide_cols(src, b)).then_inc(wide_in, 16)

        @block.gpsimd
        def _(pool):
            def split(b, g, ahead):
                t = b * GROUPS + (g + ahead)
                c = t * POOL_PER
                if rope:
                    held(pool, gate, x1_free, t + 2)
                    held(pool, gate, x2_free, x2_proj(t) + 2)
                    nc.gpsimd.tensor_tensor(qk[:, :], part1[:, :], part2[:, :], ALU.add).then_inc(pool_chain, 1)
                held(pool, gate, copies, t * 2 + 1)
                nc.gpsimd.tensor_tensor(rest1[:, :], qk[:, :], pieces[:, 0, :], ALU.subtract).then_inc(pool_chain, 1)
                held(pool, gate, copies, t * 2 + 2)
                nc.gpsimd.tensor_tensor(pieces[:, 2, :], rest1[:, :], pieces[:, 1, :],
                                        ALU.subtract).then_inc(pool_chain, 1)

            for ahead in range(AHEAD):
                split(0, 0, ahead)
            with pool.Fori(0, BATCH) as b:
                for g in range(GROUPS):
                    if g == 2:
                        join.sub_root(pool, gate, b)
                    split(b, g, AHEAD)
                    if g == 3:
                        join.x_root(pool, gate, b, b * TPB)
                    if g == 3:
                        for n, (_, hi, lo) in enumerate(wide):
                            held(pool, gate, wide_hi, b * len(wide) + (n + 1))
                            nc.gpsimd.tensor_tensor(wide_cols(lo, b), wide_raw[n][:, :, :],
                                                    wide_cols(hi, b).bitcast(F32), ALU.subtract).then_inc(wide_lo, 1)
            join.sub_root(pool, gate, BATCH)
            join.x_root(pool, gate, BATCH, BATCH * TPB)

        @block.scalar
        def _(act):
            act.sem_inc(exps, 2)
            act.sem_inc(wide_lo, 1)
            act.sem_inc(pv_copied, 1)
            act.sem_inc(m_free, 1)
            if not rope:
                act.sem_inc(x1_free, 1)

            def y_evac(use, c):
                act.wait_ge(m_full, use + 1)
                if rope:
                    nc.scalar.mul(y_t[:, c, :], ps_m[:, :], rms_w[:, c:c + 1]).then_inc(m_free, 1)
                else:
                    nc.scalar.copy(y_t[:, c, :], ps_m[:, :]).then_inc(m_free, 1)

            def rows_evac(use, slot):
                act.wait_ge(m_full, use + 1)
                nc.scalar.copy(q_st[slot][SROWS:SROWS + PIECES, 0:2, :],
                               ps_m[:, :].bitcast(BF16)[SROWS:SROWS + PIECES, :].rearrange(
                                   "p (h s) -> p h s", h=2)).then_inc(m_free, 1)

            def first_part(t):
                if rope:
                    act.wait_ge(pool_chain, t * POOL_PER + 1)
                else:
                    act.wait_ge(x1_free, t + 2)
                if not isinstance(t, int) or t > 0:
                    act.wait_ge(pieces_out, t * OUT_INC)
                nc.scalar.copy(pieces[:, 0, :], qk[:, :]).then_inc(copies, 1)

            def second_part(t):
                act.wait_ge(pool_chain, t * POOL_PER + (POOL_PER - 1))
                nc.scalar.copy(pieces[:, 1, :], rest1[:, :]).then_inc(copies, 1)

            def x1_evac(t):
                act.wait_ge(x1_full, t + 1)
                if not isinstance(t, int) or t > 0:
                    act.wait_ge(pool_chain, t * POOL_PER)
                nc.scalar.copy(part1[:, :], ps_x1[:, :]).then_inc(x1_free, 1)

            def ot_evac(use, c):
                act.wait_ge(m_full, use + 1)
                nc.scalar.copy(o_t[:, c, :], ps_m[:, :]).then_inc(m_free, 1)

            if rope:
                act.wait_ge(weights_in, 16 * 11)
            for c in range(KC):
                y_evac(c, c)
            for t in range(AHEAD):
                if not rope:
                    x1_evac(t)
                first_part(t)
                second_part(t)
            with act.Fori(0, BATCH) as b:
                for g in range(GROUPS):
                    t = b * GROUPS + g
                    rows_evac(m_use(b, g, "max"), g)
                    if g == 0 and not rope:
                        for i in range(2):
                            act.wait_ge(m_full, m_use(b, 0, f"v{i}") + 1)
                            nc.scalar.copy(v[:, 2 * i:2 * i + 2, :, 0:HD],
                                           ps_m[:, :].rearrange("p (i h d) -> p i h d", i=2, d=HD)).then_inc(m_free, 1)
                    if not rope:
                        x1_evac(t + AHEAD)
                    if g == 1:
                        for c in range(KC):
                            ot_evac(m_use(b, 1, f"ot{c}"), c)
                    for k in range(UNITS):
                        if g == 2 and k in (4, 8) and wide:
                            n = k // 4 - 1
                            act.wait_ge(wide_in, b * 32 + 32)
                            nc.scalar.copy(wide_cols(wide[n][1], b), wide_raw[n][:, :, :]).then_inc(wide_hi, 1)
                        act.wait_ge(b_full, t * UNITS + (k + 1))
                        if k == 0:
                            act.wait_ge(pv_done, t + 2)
                        nc.scalar.activation(probs[:, k, :], ps_b[k % 2][:, :], ACT.Exp,
                                             scale=scale).then_inc(exps, 1)
                        if k == 1:
                            first_part(t + AHEAD)
                        if k == 4:
                            second_part(t + AHEAD)
                    act.wait_ge(pv_done, t + 3)
                    act.wait_ge(m_full, m_use(b, g, "o") + 1)
                    nc.scalar.copy(pv_sb[:, :], ps_pv[:, :]).then_inc(pv_copied, 1)
                    if g == 0:
                        for c in range(KC):
                            y_evac(m_use(b, 0, f"yt{c}"), c)
            for c in range(KC):
                ot_evac(BATCH * M_PER + M_PRO + 1 + c, c)

        @block.tensor
        def _(pe):
            pe.sem_inc(pv_done, 2)

            def y_transposes(use, b1, c):
                pe.wait_ge(y_ready, b1 * TPB + TPB)
                pe.wait_ge(m_free, use + 1)
                for i in range(TPB):
                    last = nc.tensor.transpose(ps_m[:, i * P:(i + 1) * P], y_tok[:, i, c * P:(c + 1) * P], ident[:, :])
                last.then_inc(m_full, 1)

            def project(t, g, y_uses):
                pe.wait_ge(m_free, y_uses + 2)
                banks = ((w_x1, ps_x1, x1_full, x1_free, t), (w_x2, ps_x2, x2_full, x2_free, x2_proj(t))) \
                    if rope else ((w_x1, ps_x1, x1_full, x1_free, t),)
                for wt, ps, full, free, use in banks:
                    pe.wait_ge(free, use + 1)
                    for c in range(KC):
                        last = nc.tensor.matmul(ps[:, :], wt[:, c, g, :], y_t[:, c, :],
                                                start=(c == 0), stop=(c == KC - 1))
                    last.then_inc(full, 1)

            def mask(ps, lo, m):
                return nc.tensor.matmul(ps[:, lo:lo + P], identb[:, :], m[:, :], start=False, stop=True)

            def max_unit(t, slot, k):
                ps = ps_a[k % 2]
                pe.wait_ge(maxes, t * UNITS + (k + 1))
                if k < 4:
                    work = [(k, 3, 0)]
                elif k < 8:
                    work = [(k - 4, 2, 0), (k - 4, 0, 3 * P)]
                else:
                    work = [(2 * (k - 8), 1, 0), (2 * (k - 8) + 1, 1, 2 * P)]
                for h, i, at in work:
                    wd = (i + 1) * P
                    nc.tensor.matmul(ps[:, at:at + wd], q_st[slot][0:SROWS, h, i * P:(i + 1) * P],
                                     k_st[slot][0:SROWS, h, 0:wd], start=True, stop=False)
                    last = mask(ps, at + i * P, mask_q)
                last.then_inc(a_full, 1)

            def prob_unit(t, slot, k):
                ps = ps_b[k % 2]
                pe.wait_ge(exps, t * UNITS + (k + 1))
                if k < 4:
                    work = [(k, 0, 0)]
                elif k < 8:
                    work = [(k - 4, 1, 0), (k - 4, 3, 3 * P)]
                else:
                    work = [(2 * (k - 8), 2, 0), (2 * (k - 8) + 1, 2, 2 * P)]
                for h, j, at in work:
                    wd = SEQ - j * P
                    nc.tensor.matmul(ps[:, at:at + wd], k_st[slot][0:SROWS + PIECES, h, j * P:(j + 1) * P],
                                     q_st[slot][0:SROWS + PIECES, h, j * P:SEQ], start=True, stop=False)
                    last = mask(ps, at, mask_k)
                last.then_inc(b_full, 1)

            def pv(g, j):
                for h in range(HPG):
                    lo = j * P
                    rhs = {0: probs[:, h, :], 1: probs[:, 4 + h, 0:3 * P], 3: probs[:, 4 + h, 3 * P:SEQ],
                           2: probs[:, 8 + h // 2, (h % 2) * 2 * P:(h % 2) * 2 * P + 2 * P]}[j]
                    last = nc.tensor.matmul(ps_pv[h * VW:(h + 1) * VW, lo:SEQ], v[:, j, g * HPG + h, :], rhs,
                                            start=(j == 0), stop=(j == 2), skip_group_check=True)
                return last

            def max_transposes(t, use):
                pe.wait_ge(nmax_ready, t + 1)
                for ps, full, free, n in ((ps_m, m_full, m_free, use), (ps_x2, x2_full, x2_free, x2_max(t))):
                    pe.wait_ge(free, n + 1)
                    rows = ps[:, :].bitcast(BF16)[SROWS:SROWS + PIECES, :]
                    for h in range(2):
                        for i in range(TPB):
                            last = nc.tensor.transpose(rows[:, h * SEQ + i * P:h * SEQ + (i + 1) * P],
                                                       nmax_p[:, i, h + (0 if ps is ps_m else 2), :], identb[:, :])
                    last.then_inc(full, 1)

            def o_transposes(use, copied):
                pe.wait_ge(pv_copied, copied)
                pe.wait_ge(m_free, use + 1)
                for i in range(TPB):
                    last = nc.tensor.transpose(ps_m[:, i * P:(i + 1) * P], pv_sb[:, i * P:(i + 1) * P], ident[:, :])
                last.then_inc(m_full, 1)

            def o_project(use, o_done):
                pe.wait_ge(m_free, o_done)
                for c in range(KC):
                    pe.wait_ge(m_free, use + (c + 1))
                    for i in range(TPB):
                        last = nc.tensor.transpose(ps_m[:, i * P:(i + 1) * P], o_tok[:, i, c * P:(c + 1) * P],
                                                   ident[:, :])
                    last.then_inc(m_full, 1)
                for i in range(TPB):
                    if i % 2 == 0:
                        pe.wait_ge(m_free, use + (3 + i // 2))
                    for c in range(KC):
                        last = nc.tensor.matmul(ps_m[:, (i % 2) * D:(i % 2 + 1) * D], o_t[:, c, i * P:(i + 1) * P],
                                                w_o[:, c, :], start=(c == 0), stop=(c == KC - 1))
                    if i % 2:
                        last.then_inc(m_full, 1)

            pe.wait_ge(weights_in, 16 * (11 if rope else 3))
            for c in range(KC):
                y_transposes(c, 0, c)
            for ahead in range(AHEAD):
                project(ahead, ahead, KC - 1)
            pe.wait_ge(stacked, STACK_INC)
            for k in range(UNITS):
                max_unit(0, 0, k)
            pe.wait_ge(v_const, GROUPS + 3)
            with pe.Fori(0, BATCH) as b:
                for g in range(GROUPS):
                    t = b * GROUPS + g
                    max_transposes(t, m_use(b, g, "max"))
                    if g == 0:
                        for i in range(TPB):
                            if i % 2 == 0:
                                pe.wait_ge(m_free, m_use(b, 0, f"v{i // 2}") + 1)
                            for c in range(KC):
                                last = nc.tensor.matmul(ps_m[:, (i % 2) * D:(i % 2 + 1) * D],
                                                        y_t[:, c, i * P:(i + 1) * P], w_v[:, c, :],
                                                        start=(c == 0), stop=(c == KC - 1))
                            if i % 2:
                                last.then_inc(m_full, 1)
                    project(t + AHEAD, (g + AHEAD) % GROUPS, m_use(b, 0, "yt1") if g else m_use(b, 0, "max") - 1)
                    if g == 1:
                        o_project(m_use(b, 1, "ot0"), m_use(b, 0, "o") + 2)
                    pe.wait_ge(stacked, (t + 1) * STACK_INC + STACK_INC)
                    for k in range(UNITS):
                        max_unit(t + 1, (g + 1) % GROUPS, k)
                        if k == 0:
                            pe.wait_ge(m_free, m_use(b, g, "max") + 2)
                            pe.wait_ge(x2_free, x2_max(t) + 2)
                        prob_unit(t, g, k)
                        if k == 3:
                            o_transposes(m_use(b, g, "o"), t + 1)
                        if k == 5:
                            if g == 0:
                                pe.wait_ge(m_free, m_use(b, 0, "v1") + 2)
                            pe.wait_ge(exps, t * UNITS + (2 + 4))
                            pe.wait_ge(pv_copied, t + 1)
                            pv(g, 0)
                        if k == 9:
                            pe.wait_ge(exps, t * UNITS + (2 + 8))
                            pv(g, 1)
                            pv(g, 3)
                    pe.wait_ge(exps, t * UNITS + (2 + UNITS))
                    pv(g, 2).then_inc(pv_done, 1)
                    if g == 0:
                        for c in range(KC):
                            y_transposes(m_use(b, 0, f"yt{c}"), b + 1, c)
            end = BATCH * M_PER + M_PRO
            o_transposes(end, STEPS + 1)
            o_project(end + 1, end + 2)

        @block.vector
        def _(dve):
            dve.sem_inc(maxes, 2)
            nc.vector.memset(v[:, :, :, HD:VW], 0.0).then_inc(init_done, 1)
            for g in range(GROUPS):
                nc.vector.memset(k_st[g][SROWS:P, :, :], 1.0).then_inc(v_const, 1)
            dve.wait_ge(init_done, 1)
            nc.vector.memset(v[:, :, :, HD:HD + 1], 1.0).then_inc(v_const, 1)
            nc.vector.memset(pv_sb[:, :], 1.0).then_inc(v_const, 1)
            nc.vector.memset(o_tok[:, :, :], 0.0).then_inc(v_const, 1)
            dve.sem_inc(x2_free, 1)
            if rope:
                dve.sem_inc(x1_free, 1)

            def normalise(b1, i):
                n = b1 * TPB + i
                nc.vector.tensor_scalar(y_tok[:, i, :], x[:, bass.ds(n, 1), :].rearrange("p a d -> p (a d)"),
                                        mean[:, bass.ds(n, 1)], rin[:, bass.ds(n, 1)], ALU.subtract,
                                        ALU.mult).then_inc(y_ready, 1)

            def rotate(t, g):
                if not isinstance(t, int) or t > 0:
                    dve.wait_ge(pool_chain, t * POOL_PER - (POOL_PER - 1))
                dve.wait_ge(x1_full, t + 1)
                nc.vector.scalar_tensor_tensor(part1[:, :], ps_x1[:, :], bias1[:, g:g + 1], rot1[:, :],
                                               ALU.add, ALU.mult).then_inc(x1_free, 1)
                dve.wait_ge(x2_full, x2_proj(t) + 1)
                nc.vector.scalar_tensor_tensor(part2[:, :], ps_x2[:, :], bias2[:, g:g + 1], rot2[:, :],
                                               ALU.add, ALU.mult).then_inc(x2_free, 1)

            def unit_max(t, k):
                dve.wait_ge(a_full, t * UNITS + (k + 1))
                ps = ps_a[k % 2]
                if k < 4:
                    work = [(nmax[:, 3, k:k + 1], ps[:, :])]
                elif k < 8:
                    work = [(nmax[:, 2, k - 4:k - 3], ps[:, 0:3 * P]), (nmax[:, 0, k - 4:k - 3], ps[:, 3 * P:SEQ])]
                else:
                    work = [(nmax[:, 1, 2 * (k - 8):2 * (k - 8) + 2], ps[:, :].rearrange("p (h n) -> p h n", h=2))]
                for out, src in work:
                    last = nc.vector.tensor_reduce(out, src, AX_X, ALU.max, negate=True)
                last.then_inc(maxes, 1)

            def rows_evac(t, slot):
                dve.wait_ge(x2_full, x2_max(t) + 1)
                nc.vector.tensor_copy(q_st[slot][SROWS:SROWS + PIECES, 2:4, :],
                                      ps_x2[:, :].bitcast(BF16)[SROWS:SROWS + PIECES, :].rearrange(
                                          "p (h s) -> p h s", h=2)).then_inc(x2_free, 1)

            def max_parts(t):
                dve.wait_ge(maxes, t * UNITS + (2 + UNITS))
                c = t * 3
                flat = lambda a: a[:, :, :].rearrange("p i h -> p (i h)")
                part = lambda r: nmax_p[:, :, :, r].rearrange("p i h -> p (i h)")
                nc.vector.tensor_copy(part(0), flat(nmax)).then_inc(dve_chain, 1)
                dve.wait_ge(dve_chain, c + 1)
                nc.vector.tensor_tensor(flat(nrest), flat(nmax), part(0), ALU.subtract).then_inc(dve_chain, 1)
                dve.wait_ge(dve_chain, c + 2)
                nc.vector.tensor_copy(part(1), flat(nrest)).then_inc(dve_chain, 1)
                dve.wait_ge(dve_chain, c + 3)
                nc.vector.tensor_tensor(part(2), flat(nrest), part(1), ALU.subtract).then_inc(nmax_ready, 1)

            def o_norm(use, g, n):
                dve.wait_ge(m_full, use + 1)
                ps = ps_m[:, :].rearrange("p (i h c) -> p i h c", h=HPG, c=VW)
                nc.vector.reciprocal(rsum[:, :, :], ps[:, :, :, HD]).then_inc(rsum_ready, 1)
                dve.wait_ge(rsum_ready, n)
                nc.vector.tensor_tensor(
                    o_tok[:, :, g * HPG * HD:(g + 1) * HPG * HD].rearrange("p i (h d) -> p i h d", d=HD),
                    ps[:, :, :, 0:HD],
                    rsum[:, :, :].unsqueeze(3).to_broadcast([P, TPB, HPG, HD]), ALU.mult).then_inc(m_free, 1)

            def out_evac(use, b0, half, rn):
                dve.wait_ge(m_full, use + 1)
                n = b0 * TPB + 2 * half
                dst = sub[:, bass.ds(n, 2), :]
                src = ps_m[:, :].rearrange("p (i d) -> p i d", i=2)
                if rope:
                    for i in range(2):
                        xn = x[:, bass.ds(n + i, 1), :].rearrange("p a d -> p (a d)")
                        nc.vector.tensor_scalar(resid[:, i, :], xn, mean[:, bass.ds(n + i, 1)],
                                                rstd[:, bass.ds(n + i, 1)], ALU.subtract, ALU.mult)\
                            .then_inc(out_chain, 1)
                    dve.wait_ge(out_chain, rn * 3 + 2)
                    nc.vector.tensor_tensor(resid[:, :, :], resid[:, :, :],
                                            bias_o[:, :].unsqueeze(1).to_broadcast([P, 2, D]), ALU.add)\
                        .then_inc(out_chain, 1)
                    dve.wait_ge(out_chain, rn * 3 + 3)
                    nc.vector.tensor_tensor(dst, src, resid[:, :, :], ALU.add).then_inc(m_free, 1)
                else:
                    nc.vector.tensor_copy(dst, src).then_inc(m_free, 1)

            for i in range(TPB):
                normalise(PADT // TPB, i)
            if rope:
                dve.wait_ge(weights_in, 16 * 11)
                for ahead in range(AHEAD):
                    rotate(ahead, ahead)
            for k in range(UNITS):
                unit_max(0, k)
            max_parts(0)
            with dve.Fori(0, BATCH) as b:
                for g in range(GROUPS):
                    t = b * GROUPS + g
                    rows_evac(t, g)
                    if g == 0 and rope:
                        for i in range(2):
                            dve.wait_ge(m_full, m_use(b, 0, f"v{i}") + 1)
                            nc.vector.tensor_tensor(v[:, 2 * i:2 * i + 2, :, 0:HD],
                                                    ps_m[:, :].rearrange("p (i h d) -> p i h d", i=2, d=HD),
                                                    bias_v[:, :].rearrange("p (h d) -> p h d", d=HD).unsqueeze(1)
                                                    .to_broadcast([P, 2, HEADS, HD]), ALU.add).then_inc(m_free, 1)
                    if rope:
                        rotate(t + AHEAD, (g + AHEAD) % GROUPS)
                    if g == 1:
                        for half in range(2):
                            out_evac(m_use(b, 1, f"out{half}"), b, half, b * 2 + half)
                    for k in range(UNITS):
                        unit_max(t + 1, k)
                        if g == 0 and k >= 5 and k < 5 + TPB:
                            normalise(b + 2, k - 5)
                        if k == 4:
                            o_norm(m_use(b, g, "o"), (g - 1) % GROUPS, t + 1)
                        if g == 1 and k >= 5 and k < 5 + TPB:
                            join.stats_of(sub, b * TPB, k - 5)
                        if g == 1 and k == 9:
                            join.sub_variance(dve, b)
                        if g == 2 and k >= 5 and k < 5 + TPB:
                            join.normalise_tile(dve, b, b * TPB, k - 5)
                        if g == 2 and k == 9:
                            join.add(dve, b, b * TPB)
                        if g == 3 and k < TPB:
                            join.stats_of(x, b * TPB, k)
                        if g == 3 and k == 5:
                            join.x_variance(dve, b, b * TPB)
                    max_parts(t + 1)
            end = BATCH * M_PER + M_PRO
            o_norm(end, GROUPS - 1, STEPS + 1)
            for half in range(2):
                out_evac(end + (3 + half), BATCH, half, 2 * BATCH + half)
            dve.wait_ge(m_free, end + 6)
            join.all_on_vector(dve, BATCH, BATCH * TPB)


def setup_phase(nc, keep, x_in):
    x, ident, identb = keep["x"], keep["ident"], keep["identb"]
    with ExitStack() as ctx:
        filled, built = ctx.enter_context(nc.semaphore("filled")), ctx.enter_context(nc.semaphore("built"))
        block = ctx.enter_context(nc.Block())

        @block.sync
        def _(sp):
            for b in range(BATCH):
                sp.dma_start(x[:, PADT + b * TPB:PADT + (b + 1) * TPB, :],
                             x_in[b].rearrange("(n p) d -> p n d", p=P)).then_inc(keep["x_loaded"][b], 16)

        @block.gpsimd
        def _(pool):
            nc.gpsimd.memset(x[:, PADT + TILES:XT, :], 0.0).then_inc(built, 1)
            nc.gpsimd.memset(keep["minus_half"][:, :], -0.5).then_inc(built, 1)
            fills = ((ident, 0.0), (identb, 0.0), (keep["mask_q"], 0.0), (keep["mask_k"], 0.0))
            for buf, value in fills:
                nc.gpsimd.memset(buf[:, :], value).then_inc(filled, 1)
            pool.wait_ge(filled, len(fills))
            for m in (ident, identb):
                nc.gpsimd.affine_select(out=m[:, :], in_=m[:, :], compare_op=ALU.not_equal, fill=1.0, base=0,
                                        pattern=[[-1, P]], channel_multiplier=1).then_inc(built, 1)
            nc.gpsimd.affine_select(out=keep["mask_q"][:, :], in_=keep["mask_q"][:, :], compare_op=ALU.is_ge, fill=NEG,
                                    base=0, pattern=[[-1, P]], channel_multiplier=1).then_inc(built, 1)
            nc.gpsimd.affine_select(out=keep["mask_k"][:, :], in_=keep["mask_k"][:, :], compare_op=ALU.is_ge, fill=NEG,
                                    base=0, pattern=[[1, P]], channel_multiplier=-1).then_inc(built, 1)

        @block.vector
        def _(dve):
            for name, value in (("mean", 0.0), ("rstd", 1.0), ("rin", 1.0)):
                nc.vector.memset(keep[name][:, :], value)
            nc.vector.memset(x[:, 0:PADT, :], 0.0)
            nc.vector.memset(keep["sub"][:, 0:PADT, :], 0.0)


def norm_phase(nc, keep, dispatched):
    x, mean, rstd, rin = keep["x"], keep["mean"], keep["rstd"], keep["rin"]
    lo, hi = PADT, PADT + TILES
    with ExitStack() as ctx:
        def sb(n, shape, dt=F32):
            return ctx.enter_context(nc.sbuf_tensor(f"norm_{n}", shape, dt))

        def sem(n):
            return ctx.enter_context(nc.semaphore(f"norm_{n}"))

        stats = sb("stats", [P, TILES, 6])
        moments = sb("moments", [P, TILES, 2])
        var_eps, mean_sq = sb("var_eps", [P, TILES]), sb("mean_sq", [P, TILES])
        minus_half = keep["minus_half"]
        chain, var_ready, root_ready = sem("chain"), sem("var_ready"), sem("root_ready")
        block = ctx.enter_context(nc.Block())

        @block.sync
        def _(sp):
            for e in range(E0 + 1):
                slots = dispatched[e * CAP:(e + 1) * CAP, :].rearrange("(p t) d -> p t d", t=CT)
                for t in range(0, CT, PADT):
                    n = min(PADT, CT - t)
                    sp.dma_start(slots[:, t:t + n, :], x[:, PADT + TILES:PADT + TILES + n, :])\
                      .then_inc(keep["cleared"], 16)

        @block.gpsimd
        def _(pool):
            for r, out in enumerate((rstd, rin)):
                pool.wait_ge(var_ready, r + 1)
                nc.gpsimd.tensor_tensor(out[:, lo:hi], var_eps[:, :], minus_half[:, :].to_broadcast([P, TILES]),
                                        ALU.pow).then_inc(root_ready, 1)

        @block.vector
        def _(dve):
            done = [0]

            def after(ins):
                done[0] += 1
                ins.then_inc(chain, 1)
                dve.wait_ge(chain, done[0])

            for n in range(TILES):
                if n % TPB == 0:
                    dve.wait_ge(keep["x_loaded"][n // TPB], 16)
                last = nc.vector.bn_stats(stats[:, n, :], x[:, lo + n, :])
            after(last)
            for n in range(TILES):
                last = nc.vector.bn_aggr(moments[:, n, :], stats[:, n, :])
            after(last)
            nc.vector.tensor_scalar(var_eps[:, :], moments[:, :, 1], EPS, None, ALU.add).then_inc(var_ready, 1)
            after(nc.vector.tensor_copy(mean[:, lo:hi], moments[:, :, 0]))
            dve.wait_ge(root_ready, 1)
            after(nc.vector.tensor_tensor(mean_sq[:, :], moments[:, :, 1], rstd[:, lo:hi], ALU.mult))
            after(nc.vector.tensor_tensor(mean_sq[:, :], mean_sq[:, :], rstd[:, lo:hi], ALU.mult))
            nc.vector.tensor_scalar(var_eps[:, :], mean_sq[:, :], EPS, None, ALU.add).then_inc(var_ready, 1)
            dve.wait_ge(root_ready, 2)
            after(nc.vector.tensor_tensor(rin[:, lo:hi], rin[:, lo:hi], rstd[:, lo:hi], ALU.mult))


def keep_all(nc, ctx):
    def sb(name, shape, dt=F32):
        return ctx.enter_context(nc.sbuf_tensor(f"kept_{name}", shape, dt))
    return {"x": sb("x", [P, XT, D]), "sub": sb("sub", [P, XT, D]), "mean": sb("mean", [P, XT]),
            "rstd": sb("rstd", [P, XT]), "rin": sb("rin", [P, XT]), "ident": sb("ident", [P, P]),
            "identb": sb("identb", [P, P], BF16), "mask_q": sb("mask_q", [P, P], BF16),
            "mask_k": sb("mask_k", [P, P], BF16), "minus_half": sb("minus_half", [P, 1]),
            "gate": ctx.enter_context(nc.semaphore("gate"))}


def rotation_tables():
    d = np.arange(P) // HPG % HD
    freqs = np.float32(10000.0) ** ((d % (HD // 2)).astype(np.float32) * np.float32(-2.0 / HD))
    ang = (np.arange(SEQ, dtype=np.float32)[None, :] * freqs[:, None].astype(np.float32)).astype(np.float32)
    even = (d % 2 == 0)[:, None]
    cos, sin = np.cos(ang), np.sin(ang)
    return (np.where(even, cos, sin).astype(np.float32), np.where(even, -sin, cos).astype(np.float32))


def stack_columns(wq, wk, order):
    def cols(a):
        heads = a.reshape(a.shape[0], GROUPS, HPG, HD)[..., order]
        return heads.transpose(0, 1, 3, 2).reshape(a.shape[0], GROUPS, HD * HPG)
    return np.concatenate([cols(wq), cols(wk)], axis=2)


def chunked(a):
    return np.ascontiguousarray(np.moveaxis(a.reshape(a.shape[0] // P, P, *a.shape[1:]), 0, 1))


def route_phase(nc, keep, w, route, w1):
    x, sub, mean, rstd, ident = keep["x"], keep["sub"], keep["mean"], keep["rstd"], keep["ident"]
    with ExitStack() as ctx:
        def sb(n, shape, dt=F32):
            return ctx.enter_context(nc.sbuf_tensor(f"route_{n}", shape, dt))

        def psum(n, shape, dt=F32):
            return ctx.enter_context(nc.psum_tensor(f"route_{n}", shape, dt))

        def sem(n):
            return ctx.enter_context(nc.semaphore(f"route_{n}"))

        w_g = sb("w_g", [P, KC, E0])
        y_tok, y_t = sb("y_tok", [P, TPB, D]), sb("y_t", [P, KC, SEQ])
        logits, shifted, expd = sb("logits", [P, TILES, E0]), sb("shifted", [P, TILES, E0]), sb("expd", [P, TILES, E0])
        top, top_shift, top_exp = sb("top", [P, TILES, 8]), sb("top_shift", [P, TILES, 2]), sb("top_exp", [P, TILES, 2])
        top_at, top_atf = sb("top_at", [P, TILES, 8], U32), sb("top_atf", [P, TILES, 2])
        total, inv_total = sb("total", [P, TILES]), sb("inv_total", [P, TILES])
        numbers = sb("numbers", [P, E0])
        hot = sb("hot", [P, 2, TILES, E0])
        hot_sum = sb("hot_sum", [P, TILES, E0], BF16)
        before, ones = sb("before", [P, P], BF16), sb("ones", [P, P], BF16)
        ranks = sb("ranks", [P, TILES, E0])
        picked = sb("picked", [P, 2, TILES, E0])
        rank, kept, slot = sb("rank", [P, 2, TILES]), sb("kept", [P, 2, TILES]), sb("slot", [P, 2, TILES])
        far = sb("far", [P, 2, TILES])
        put_at = sb("put_at", [P, 2, TILES], U32)
        ps_t = [psum(f"ps_t{i}", [P, SEQ]) for i in range(2)]
        ps_l = psum("ps_l", [P, TPB, E0])
        ps_r = psum("ps_r", [P, TILES, E0])

        w_in, consts = sem("w_in"), sem("consts")
        y_ready, y_kept = sem("y_ready"), sem("y_kept")
        t_full, t_free, l_full, l_free = sem("t_full"), sem("t_free"), sem("l_full"), sem("l_free")
        chain, to_exp, exp_done = sem("chain"), sem("to_exp"), sem("exp_done")
        hot_ready, ranks_ready, slots_ready, scattered = (sem("hot_ready"), sem("ranks_ready"), sem("slots_ready"),
                                                          sem("scattered"))
        first_in, first_hi, first_lo = sem("first_in"), sem("first_hi"), sem("first_lo")
        block = ctx.enter_context(nc.Block())

        @block.sync
        def _(sp):
            sp.dma_start(w_g[:, :, :], w["g"]).then_inc(w_in, 16)
            sp.dma_start(w1["raw"][:, :, :], w["w1"][0].rearrange("(c p) f -> p c f", p=P)).then_inc(first_in, 16)
            sp.wait_ge(w_in, 16)

        @block.gpsimd
        def _(pool):
            nc.gpsimd.iota(numbers[:, :], [[1, E0]], base=0, channel_multiplier=0,
                           allow_small_or_imprecise_dtypes=True).then_inc(consts, 1)
            nc.gpsimd.memset(ones[:, :], 1.0).then_inc(consts, 1)
            nc.gpsimd.memset(before[:, :], 1.0).then_inc(consts, 1)
            pool.wait_ge(consts, 3)
            nc.gpsimd.affine_select(out=before[:, :], in_=before[:, :], compare_op=ALU.is_gt, fill=0.0, base=0,
                                    pattern=[[1, P]], channel_multiplier=-1).then_inc(consts, 1)
            pool.wait_ge(first_hi, 1)
            nc.gpsimd.tensor_tensor(w1["lo"][:, :, :], w1["raw"][:, :, :], w1["hi"][:, :, :].bitcast(F32),
                                    ALU.subtract).then_inc(first_lo, 1)
            pool.wait_ge(slots_ready, 1)
            pool.wait_ge(keep["cleared"], 16 * (E0 + 1) * -(-CT // PADT))
            pool.wait_ge(y_kept, TILES)
            for k in range(2):
                for n in range(TILES):
                    nc.gpsimd.indirect_dma_start(
                        out=w["dispatched"][:, :],
                        out_offset=bass.IndirectOffsetOnAxis(ap=put_at[:, k, n:n + 1], axis=0),
                        in_=sub[:, PADT + n, :], in_offset=None, bounds_check=SLOTS - 1,
                        oob_is_err=False).then_inc(scattered, 16)
            pool.wait_ge(scattered, 16 * 2 * TILES)

        @block.scalar
        def _(act):
            act.sem_inc(t_free, 2)
            with act.Fori(0, BATCH) as b:
                for c in range(KC):
                    act.wait_ge(t_full, b * KC + (c + 1))
                    nc.scalar.copy(y_t[:, c, :], ps_t[c][:, :]).then_inc(t_free, 1)
            act.wait_ge(first_in, 16)
            nc.scalar.copy(w1["hi"][:, :, :], w1["raw"][:, :, :]).then_inc(first_hi, 1)
            act.wait_ge(to_exp, 2)
            nc.scalar.activation(expd[:, :, :], shifted[:, :, :], ACT.Exp).then_inc(exp_done, 1)
            nc.scalar.activation(top_exp[:, :, :], top_shift[:, :, :], ACT.Exp).then_inc(exp_done, 1)

        @block.tensor
        def _(pe):
            pe.sem_inc(l_free, 1)
            pe.wait_ge(w_in, 16)
            with pe.Fori(0, BATCH) as b:
                for c in range(KC):
                    pe.wait_ge(y_ready, b * TPB + TPB)
                    pe.wait_ge(t_free, b * KC + (c + 1))
                    for i in range(TPB):
                        last = nc.tensor.transpose(ps_t[c][:, i * P:(i + 1) * P], y_tok[:, i, c * P:(c + 1) * P],
                                                   ident[:, :])
                    last.then_inc(t_full, 1)
                pe.wait_ge(t_free, b * KC + (KC + 2))
                pe.wait_ge(l_free, b + 1)
                for i in range(TPB):
                    for c in range(KC):
                        last = nc.tensor.matmul(ps_l[:, i, :], y_t[:, c, i * P:(i + 1) * P], w_g[:, c, :],
                                                start=(c == 0), stop=(c == KC - 1))
                last.then_inc(l_full, 1)
            pe.wait_ge(consts, 4)
            pe.wait_ge(hot_ready, 1)
            for n in range(TILES):
                nc.tensor.matmul(ps_r[:, n, :], before[:, :], hot_sum[:, n, :], start=(n == 0), stop=True,
                                 skip_group_check=True)
            for n in range(TILES - 1):
                last = nc.tensor.matmul(ps_r[:, n + 1:TILES, :], ones[:, :],
                                        hot_sum[:, n:n + 1, :].to_broadcast([P, TILES - 1 - n, E0]),
                                        start=False, stop=True, skip_group_check=True)
            last.then_inc(ranks_ready, 1)

        @block.vector
        def _(dve):
            done = [0]

            def after(ins):
                done[0] += 1
                ins.then_inc(chain, 1)
                dve.wait_ge(chain, done[0])

            with dve.Fori(0, BATCH) as b:
                for i in range(TPB):
                    n = b * TPB + (PADT + i)
                    if i == 0:
                        dve.wait_ge(t_free, b * KC + 2)
                    xn = x[:, bass.ds(n, 1), :].rearrange("p a d -> p (a d)")
                    nc.vector.tensor_scalar(y_tok[:, i, :], xn, mean[:, bass.ds(n, 1)], rstd[:, bass.ds(n, 1)],
                                            ALU.subtract, ALU.mult).then_inc(y_ready, 1)
                    nc.vector.tensor_scalar(sub[:, bass.ds(n, 1), :].rearrange("p a d -> p (a d)"), xn,
                                            mean[:, bass.ds(n, 1)], rstd[:, bass.ds(n, 1)], ALU.subtract,
                                            ALU.mult).then_inc(y_kept, 1)
                dve.wait_ge(l_full, b + 1)
                nc.vector.tensor_copy(logits[:, bass.ds(b * TPB, TPB), :], ps_l[:, :, :]).then_inc(l_free, 1)
            dve.wait_ge(l_free, BATCH + 1)
            for n in range(TILES):
                last = nc.vector.max(top[:, n, :], logits[:, n, :])
            after(last)
            for n in range(TILES):
                last = nc.vector.max_index(top_at[:, n, :], top[:, n, :], logits[:, n, :])
            after(last)
            peak = top[:, :, 0:1]
            nc.vector.tensor_tensor(shifted[:, :, :], logits[:, :, :], peak.to_broadcast([P, TILES, E0]),
                                    ALU.subtract).then_inc(to_exp, 1)
            nc.vector.tensor_tensor(top_shift[:, :, :], top[:, :, 0:2], peak.to_broadcast([P, TILES, 2]),
                                    ALU.subtract).then_inc(to_exp, 1)
            after(nc.vector.tensor_copy(top_atf[:, :, :], top_at[:, :, 0:2]))
            dve.wait_ge(consts, 1)
            for k in range(2):
                after(nc.vector.tensor_tensor(hot[:, k, :, :], numbers[:, :].unsqueeze(1).to_broadcast([P, TILES, E0]),
                                              top_atf[:, :, k:k + 1].to_broadcast([P, TILES, E0]), ALU.is_equal))
            nc.vector.tensor_tensor(hot_sum[:, :, :], hot[:, 0, :, :], hot[:, 1, :, :], ALU.add).then_inc(hot_ready, 1)
            dve.wait_ge(exp_done, 2)
            after(nc.vector.tensor_reduce(total[:, :], expd[:, :, :], AX_X, ALU.add))
            after(nc.vector.reciprocal(inv_total[:, :], total[:, :]))
            gates = route["gates"]
            for k in range(2):
                after(nc.vector.tensor_tensor(gates[:, k, :], top_exp[:, :, k], inv_total[:, :], ALU.mult))
            dve.wait_ge(ranks_ready, 1)
            after(nc.vector.tensor_copy(ranks[:, :, :], ps_r[:, :, :]))
            for k in range(2):
                after(nc.vector.tensor_tensor(picked[:, k, :, :], hot[:, k, :, :], ranks[:, :, :], ALU.mult))
            after(nc.vector.tensor_reduce(rank[:, :, :], picked[:, :, :, :], AX_X, ALU.add))
            after(nc.vector.tensor_scalar(kept[:, :, :], rank[:, :, :], float(CAP), None, ALU.is_lt))
            for k in range(2):
                after(nc.vector.scalar_tensor_tensor(slot[:, k, :], top_atf[:, :, k], float(CAP), rank[:, k, :],
                                                     ALU.mult, ALU.add))
            after(nc.vector.tensor_scalar(far[:, :, :], kept[:, :, :], -2.0 * SLOTS, 2.0 * SLOTS, ALU.mult, ALU.add))
            after(nc.vector.tensor_tensor(far[:, :, :], far[:, :, :], slot[:, :, :], ALU.add))
            after(nc.vector.tensor_copy(put_at[:, :, :], far[:, :, :]))
            dve.sem_inc(slots_ready, 1)
            after(nc.vector.tensor_tensor(slot[:, :, :], slot[:, :, :], kept[:, :, :], ALU.mult))
            after(nc.vector.tensor_copy(route["get_at"][:, :, :], slot[:, :, :]))
            after(nc.vector.tensor_tensor(gates[:, :, :], gates[:, :, :], kept[:, :, :], ALU.mult))


def expert_phase(nc, keep, w, w1, w2):
    ident = keep["ident"]
    PAIR = 2
    HALF = CAP // 2
    U_FILLS, T_FILLS, O_FILLS = 2 * FC, -(-KC * CT // 4), -(-CT // 2)
    U_BANKS, T_BANKS, O_BANKS = 4, 2, 2
    W2_AT = 5
    with ExitStack() as ctx:
        def sb(n, shape, dt=F32):
            return ctx.enter_context(nc.sbuf_tensor(f"exp_{n}", shape, dt))

        def sem(n):
            return ctx.enter_context(nc.semaphore(f"exp_{n}"))

        def banks(n, count):
            return [ctx.enter_context(nc.psum_tensor(f"exp_ps_{n}{i}", [P, SEQ], F32)) for i in range(count)]

        rows = [sb(f"rows{i}", [P, CT, D]) for i in range(PAIR)]
        x_t = [sb(f"x_t_{n}", [P, KC * CAP], F32R) for n in ("hi", "lo")]
        h = [sb(f"h_{n}", [P, FC, CAP], F32R) for n in ("hi", "lo")]
        out = [sb(f"out{i}", [P, CT * D]) for i in range(PAIR)]
        ps_u, ps_t, ps_o = banks("u", U_BANKS), banks("t", T_BANKS), banks("o", O_BANKS)

        rows_in, stored = [[sem(f"{n}{i}") for i in range(PAIR)] for n in ("rows_in", "stored")]
        w1_in, w2_in = sem("w1_in"), sem("w2_in")
        u_full, u_hi, u_free = sem("u_full"), sem("u_hi"), sem("u_free")
        t_full, t_hi, t_free = sem("t_full"), sem("t_hi"), sem("t_free")
        o_full, o_free = sem("o_full"), sem("o_free")
        w1_hi_ready, w2_hi_ready = sem("w1_hi_ready"), sem("w2_hi_ready")
        w1_ready, w2_ready = sem("w1_ready"), sem("w2_ready")
        gate = keep["gate"]
        dispatched, results = w["dispatched"], w["results"]

        def fills(it, p, per, n):
            return it * (PAIR * per) + (p * per + n)

        def t_block(n):
            width = min(SEQ, KC * CAP - n * SEQ)
            return slice(0, width), slice(n * SEQ, n * SEQ + width)

        def load_rows(sp, e, p):
            sp.dma_start(rows[p][:, :, :], dispatched[bass.ds(e * CAP, CAP), :].rearrange(
                "(p t) d -> p t d", t=CT)).then_inc(rows_in[p], 16)

        def load_weights(sp, name, to, loaded, e):
            sp.dma_start(to["raw"][:, :, :], w[name][bass.ds(e, 1), :, :].rearrange(
                "e (c p) f -> p (e c) f", p=P)).then_inc(loaded, 16)

        def store(sp, it, p):
            held(sp, gate, o_free, fills(it, p, O_FILLS, O_FILLS + O_BANKS))
            sp.dma_start(results[bass.ds((it * PAIR + p) * CAP, CAP), :].rearrange(
                "(p t) d -> p (t d)", t=CT), out[p][:, :]).then_inc(stored[p], 16)

        block = ctx.enter_context(nc.Block())

        @block.sync
        def _(sp):
            for p in range(PAIR):
                sp.sem_inc(stored[p], 16)
            load_rows(sp, 0, 0)
            load_weights(sp, "w2", w2, w2_in, 0)
            load_rows(sp, 1, 1)
            load_weights(sp, "w1", w1, w1_in, 1)
            sp.wait_ge(t_full, T_FILLS)
            load_rows(sp, 2, 0)
            with sp.Fori(0, E0 // PAIR - 1) as it:
                for p in range(PAIR):
                    e = it * PAIR + p
                    held(sp, gate, w2_ready, e + 1)
                    load_weights(sp, "w2", w2, w2_in, e + 1)
                    held(sp, gate, t_full, fills(it, p, T_FILLS, 2 * T_FILLS))
                    load_rows(sp, e + 3, 1 - p)
                    held(sp, gate, w1_ready, e + 2)
                    load_weights(sp, "w1", w1, w1_in, e + 2)
                    store(sp, it, p)
            sp.wait_ge(w2_ready, E0 - 1)
            load_weights(sp, "w2", w2, w2_in, E0 - 1)
            sp.wait_ge(w1_ready, E0)
            sp.sem_inc(w1_in, 16)
            for p in range(PAIR):
                store(sp, E0 // PAIR - 1, p)
            for p in range(PAIR):
                sp.wait_ge(stored[p], 16 * (E0 // PAIR + 1))

        @block.gpsimd
        def _(pool):
            pool.sem_inc(w1_ready, 1)

            def lower(of, hi_ready, count, ready):
                held(pool, gate, hi_ready, count)
                nc.gpsimd.tensor_tensor(of["lo"][:, :, :], of["raw"][:, :, :], of["hi"][:, :, :].bitcast(F32),
                                        ALU.subtract).then_inc(ready, 1)

            with pool.Fori(0, E0 // PAIR) as it:
                for p in range(PAIR):
                    lower(w2, w2_hi_ready, it * PAIR + (p + 1), w2_ready)
                    lower(w1, w1_hi_ready, it * PAIR + (p + 1), w1_ready)

        @block.scalar
        def _(act):
            def t_upper(it, p):
                for n in range(T_FILLS):
                    src, dst = t_block(n)
                    act.wait_ge(t_full, fills(it, p, T_FILLS, n + 1))
                    nc.scalar.copy(x_t[0][:, dst], ps_t[(p * T_FILLS + n) % T_BANKS][:, src]).then_inc(t_hi, 1)

            def upper(of, loaded, count, ready):
                act.wait_ge(loaded, count)
                nc.scalar.copy(of["hi"][:, :, :], of["raw"][:, :, :]).then_inc(ready, 1)

            t_upper(0, 0)
            with act.Fori(0, E0 // PAIR) as it:
                for p in range(PAIR):
                    for n in range(U_FILLS):
                        f, half = divmod(n, 2)
                        act.wait_ge(u_full, fills(it, p, U_FILLS, n + 1))
                        nc.scalar.activation(h[0][:, f, half * HALF:(half + 1) * HALF],
                                             ps_u[n % U_BANKS][:, 0:HALF], ACT.Relu).then_inc(u_hi, 1)
                        if n == W2_AT:
                            upper(w2, w2_in, it * 32 + 16 * (p + 1), w2_hi_ready)
                    t_upper(it, p + 1)
                    upper(w1, w1_in, it * 32 + 16 * (p + 1), w1_hi_ready)

        @block.vector
        def _(dve):
            dve.sem_inc(u_free, U_BANKS)
            dve.sem_inc(t_free, T_BANKS)
            dve.sem_inc(o_free, O_BANKS)

            def t_lower(it, p):
                for n in range(T_FILLS):
                    src, dst = t_block(n)
                    dve.wait_ge(t_hi, fills(it, p, T_FILLS, n + 1))
                    nc.vector.tensor_tensor(x_t[1][:, dst], ps_t[(p * T_FILLS + n) % T_BANKS][:, src],
                                            x_t[0][:, dst].bitcast(F32), ALU.subtract).then_inc(t_free, 1)

            t_lower(0, 0)
            with dve.Fori(0, E0 // PAIR) as it:
                for p in range(PAIR):
                    for n in range(U_FILLS):
                        f, half = divmod(n, 2)
                        cols = slice(half * HALF, (half + 1) * HALF)
                        dve.wait_ge(u_hi, fills(it, p, U_FILLS, n + 1))
                        nc.vector.scalar_tensor_tensor(h[1][:, f, cols], ps_u[n % U_BANKS][:, 0:HALF], 0.0,
                                                       h[0][:, f, cols].bitcast(F32), ALU.max,
                                                       ALU.subtract).then_inc(u_free, 1)
                    t_lower(it, p + 1)
                    for n in range(O_FILLS):
                        width = min(SEQ, CT * D - n * SEQ)
                        dve.wait_ge(o_full, fills(it, p, O_FILLS, n + 1))
                        if n == 0:
                            dve.wait_ge(stored[p], it * 16 + 16)
                        nc.vector.tensor_copy(out[p][:, n * SEQ:n * SEQ + width],
                                              ps_o[(p * O_FILLS + n) % O_BANKS][:, 0:width]).then_inc(o_free, 1)

        @block.tensor
        def _(pe):
            def transposes(it, p):
                for n in range(KC * CT):
                    if n % 4 == 0:
                        pe.wait_ge(t_free, fills(it, p, T_FILLS, n // 4 + 1))
                        bank = ps_t[(p * T_FILLS + n // 4) % T_BANKS]
                    c, t = divmod(n, CT)
                    last = nc.tensor.transpose(bank[:, n % 4 * P:(n % 4 + 1) * P],
                                               rows[p % PAIR][:, t, c * P:(c + 1) * P], ident[:, :])
                    if n % 4 == 3 or n == KC * CT - 1:
                        last.then_inc(t_full, 1)

            def hidden(it, p):
                for f in range(FC):
                    for half in range(2):
                        pe.wait_ge(u_free, fills(it, p, U_FILLS, 2 * f + half + 1))
                    for c in range(KC):
                        for n, (i, j) in enumerate(PASSES):
                            for half in range(2):
                                last = nc.tensor.matmul(ps_u[(2 * f + half) % U_BANKS][:, 0:HALF],
                                                        (w1["hi"], w1["lo"])[i][:, c, f * P:(f + 1) * P],
                                                        x_t[j][:, c * CAP + half * HALF:c * CAP + (half + 1) * HALF],
                                                        start=(c == 0 and n == 0),
                                                        stop=(c == KC - 1 and n == len(PASSES) - 1))
                                if c == KC - 1 and n == len(PASSES) - 1:
                                    last.then_inc(u_full, 1)

            def outputs(it, p):
                for t in range(CT):
                    if t % 2 == 0:
                        pe.wait_ge(o_free, fills(it, p, O_FILLS, t // 2 + 1))
                        bank = ps_o[(p * O_FILLS + t // 2) % O_BANKS]
                    for f in range(FC):
                        for n, (i, j) in enumerate(PASSES):
                            last = nc.tensor.matmul(bank[:, t % 2 * D:(t % 2 + 1) * D], h[i][:, f, t * P:(t + 1) * P],
                                                    (w2["hi"], w2["lo"])[j][:, f, :], start=(f == 0 and n == 0),
                                                    stop=(f == FC - 1 and n == len(PASSES) - 1))
                    if t % 2 or t == CT - 1:
                        last.then_inc(o_full, 1)

            pe.wait_ge(rows_in[0], 16)
            transposes(0, 0)
            with pe.Fori(0, E0 // PAIR) as it:
                for p in range(PAIR):
                    pe.wait_ge(t_free, fills(it, p, T_FILLS, T_FILLS + T_BANKS))
                    pe.wait_ge(w1_ready, it * PAIR + (p + 1))
                    hidden(it, p)
                    pe.wait_ge(rows_in[1 - p], it * 16 + 16 * (1 + p))
                    transposes(it, p + 1)
                    pe.wait_ge(u_free, fills(it, p, U_FILLS, U_FILLS + U_BANKS))
                    pe.wait_ge(w2_ready, it * PAIR + (p + 1))
                    outputs(it, p)


def combine_phase(nc, keep, w, route):
    x, sub, gates, get_at = keep["x"], keep["sub"], route["gates"], route["get_at"]
    DEEP = 6
    with ExitStack() as ctx:
        picked = [ctx.enter_context(nc.sbuf_tensor(f"comb_picked{i}", [P, 2, D], F32)) for i in range(DEEP)]
        scaled = ctx.enter_context(nc.sbuf_tensor("comb_scaled", [P, TILES, D], F32))
        gathered = [ctx.enter_context(nc.semaphore(f"comb_gathered{i}")) for i in range(DEEP)]
        scaled_done, summed = ctx.enter_context(nc.semaphore("comb_scaled_done")), ctx.enter_context(nc.semaphore("summed"))
        gate = keep["gate"]
        join = Joining(nc, ctx, keep, "comb_join")
        block = ctx.enter_context(nc.Block())

        @block.gpsimd
        def _(pool):
            for b in range(BATCH + 2):
                for n in range(b * TPB, (b + 1) * TPB) if b < BATCH else ():
                    if n >= DEEP:
                        pool.wait_ge(summed, n - DEEP + 1)
                    for k in range(2):
                        nc.gpsimd.indirect_dma_start(
                            out=picked[n % DEEP][:, k, :], out_offset=None, in_=w["results"][:, :],
                            in_offset=bass.IndirectOffsetOnAxis(ap=get_at[:, k, n:n + 1], axis=0),
                            bounds_check=SLOTS - 1, oob_is_err=False).then_inc(gathered[n % DEEP], 16)
                if b >= 1 and b <= BATCH:
                    join.sub_root(pool, gate, b - 1)
                if b >= 2:
                    join.x_root(pool, gate, b - 2, PADT + (b - 2) * TPB)

        @block.vector
        def _(dve):
            for b in range(BATCH + 2):
                for i in range(TPB) if b < BATCH else ():
                    n = b * TPB + i
                    dve.wait_ge(gathered[n % DEEP], 32 * (n // DEEP + 1))
                    nc.vector.tensor_scalar(scaled[:, n, :], picked[n % DEEP][:, 0, :], gates[:, 0, n:n + 1], None,
                                            ALU.mult).then_inc(scaled_done, 1)
                    dve.wait_ge(scaled_done, n + 1)
                    nc.vector.scalar_tensor_tensor(sub[:, PADT + n, :], picked[n % DEEP][:, 1, :],
                                                   gates[:, 1, n:n + 1], scaled[:, n, :], ALU.mult,
                                                   ALU.add).then_inc(summed, 1)
                if b >= 1 and b <= BATCH:
                    n0 = PADT + (b - 1) * TPB
                    for i in range(TPB):
                        join.normalise_tile(dve, b - 1, n0, i)
                    join.add(dve, b - 1, n0)
                    for i in range(TPB):
                        join.stats_of(x, n0, i)
                    join.x_variance(dve, b - 1, n0)
                if b < BATCH:
                    dve.wait_ge(summed, (b + 1) * TPB)
                    for i in range(TPB):
                        join.stats_of(sub, PADT + b * TPB, i)
                    join.sub_variance(dve, b)


def dense_phase(nc, keep, w, wide, out):
    x, sub, mean, rstd, ident = keep["x"], keep["sub"], keep["mean"], keep["rstd"], keep["ident"]
    NE = E1 + 1
    NR = NE + NE % 2
    with ExitStack() as ctx:
        def sb(n, shape, dt=F32):
            return ctx.enter_context(nc.sbuf_tensor(f"dense_{n}", shape, dt))

        def psum(n, shape, dt=F32):
            return ctx.enter_context(nc.psum_tensor(f"dense_{n}", shape, dt))

        def sem(n):
            return ctx.enter_context(nc.semaphore(f"dense_{n}"))

        def pair(n, shape):
            return [sb(f"{n}_{part}", shape, F32R) for part in ("hi", "lo")]

        (_, *w_gate), (_, *w_up) = wide
        w_r, w_r_raw = pair("w_r", [P, KC, NR]), sb("w_r_raw", [P, KC, NR])
        w_down, w_down_raw = pair("w_down", [P, HB, D]), sb("w_down_raw", [P, HB, D])
        y_tok, y_t = sb("y_tok", [P, TPB, D]), pair("y_t", [P, KC, SEQ])
        scores = sb("scores", [P, TPB, NE])
        top, top_at, top_atf = sb("top", [P, TPB, 8]), sb("top_at", [P, TPB, 8], U32), sb("top_atf", [P, TPB, 2])
        diff, two = sb("diff", [P, 2, TPB]), sb("two", [P, 2, TPB])
        numbers = sb("numbers", [P, E1])
        hot, mix = sb("hot", [P, 2, TPB, E1]), sb("mix", [P, TPB, NE])
        gated = [sb(f"gated{i}", [P, SEQ]) for i in range(2)]
        product = [sb(f"product{i}", [P, SEQ]) for i in range(2)]
        h = pair("h", [P, HB, SEQ])
        side, side_sum = sb("side", [P, 4, D]), sb("side_sum", [P, TPB, D])
        ps_t = [psum(f"ps_t{i}", [P, SEQ]) for i in range(KC)]
        ps_g = [psum(f"ps_g{i}", [P, SEQ]) for i in range(2)]
        ps_u = [psum(f"ps_u{i}", [P, SEQ]) for i in range(2)]
        ps_d = [psum(f"ps_d{i}", [P, SEQ]) for i in range(2)]

        y_hi, r_ready = sem("y_hi"), sem("r_ready")
        down_hi, down_lo = sem("down_hi"), sem("down_lo")
        side_read = sem("side_read")
        side_scaled, side_added, all_added = sem("side_scaled"), sem("side_added"), sem("all_added")
        product_done, h_hi = sem("product_done"), sem("h_hi")
        w_in, down_in, consts = sem("w_in"), sem("down_in"), sem("consts")
        y_ready, t_full, t_free = sem("y_ready"), sem("t_full"), sem("t_free")
        s_full, s_free = sem("s_full"), sem("s_free")
        g_full, silu_done, u_full, h_done = sem("g_full"), sem("silu_done"), sem("u_full"), sem("h_done")
        d_full, d_free = sem("d_full"), sem("d_free")
        chain, diff_ready, two_ready, gate = sem("chain"), sem("diff_ready"), sem("two_ready"), keep["gate"]
        stored = sem("stored")
        join = Joining(nc, ctx, keep, "dense_join", then_stats=False)
        block = ctx.enter_context(nc.Block())
        DOWN_AT = {3: (slice(0, HB // 2), 0), 5: (slice(HB // 2, HB), 1)}
        D_FILLS = (NE + 1) // 2
        SIDE_FILLS, MAIN_FILLS = (1, 3), (0, 2, 4)
        SIDE = [2 * k + j for k in SIDE_FILLS for j in range(2)]
        N_SIDE = len(SIDE)
        ADDS = N_SIDE - 1
        CHAIN_N = 7 + TPB * (NE - N_SIDE)

        @block.sync
        def _(sp):
            sp.dma_start(w_r_raw[:, :, :], w["r"]).then_inc(w_in, 16)
            sp.dma_start(w_down_raw[:, :, :], w["down"]).then_inc(down_in, 16)
            for b in range(BATCH):
                held(sp, gate, join.joined, b + 2)
                sp.dma_start(out[b].rearrange("(n p) d -> p n d", p=P),
                             x[:, PADT + b * TPB:PADT + (b + 1) * TPB, :]).then_inc(stored, 16)
            sp.wait_ge(stored, 16 * BATCH)

        @block.gpsimd
        def _(pool):
            nc.gpsimd.iota(numbers[:, :], [[1, E1]], base=0, channel_multiplier=0,
                           allow_small_or_imprecise_dtypes=True).then_inc(consts, 1)
            pool.sem_inc(h_done, 2)
            pool.sem_inc(side_added, ADDS)

            def batch(b):
                for n in range(HB):
                    held(pool, gate, h_hi, b * HB + (n + 1))
                    nc.gpsimd.tensor_tensor(h[1][:, n, :], product[n % 2][:, :], h[0][:, n, :].bitcast(F32),
                                            ALU.subtract).then_inc(h_done, 1)
                    if n == TPB:
                        join.sub_root(pool, gate, b)
                    if isinstance(b, int) and n in DOWN_AT:
                        cols, k = DOWN_AT[n]
                        pool.wait_ge(down_hi, k + 1)
                        nc.gpsimd.tensor_tensor(w_down[1][:, cols, :], w_down_raw[:, cols, :],
                                                w_down[0][:, cols, :].bitcast(F32), ALU.subtract).then_inc(down_lo, 1)
                held(pool, gate, all_added, b + 1)
                for i in range(TPB):
                    tile = b * TPB + i
                    for k in range(1, N_SIDE):
                        held(pool, gate, side_scaled, tile * N_SIDE + (k + 1))
                        if k > 1:
                            held(pool, gate, side_added, tile * ADDS + (ADDS + k - 1))
                        nc.gpsimd.tensor_tensor(side_sum[:, i, :], side[:, 0, :] if k == 1 else side_sum[:, i, :],
                                                side[:, k, :], ALU.add).then_inc(side_added, 1)

            batch(0)
            with pool.Fori(1, BATCH) as b:
                batch(b)
            join.sub_root(pool, gate, BATCH)

        @block.scalar
        def _(act):
            act.sem_inc(silu_done, 2)
            act.sem_inc(side_read, 1)

            def upper(b, n):
                act.wait_ge(product_done, b * HB + (2 + n + 1))
                nc.scalar.copy(h[0][:, n, :], product[n % 2][:, :]).then_inc(h_hi, 1)

            def batch(b):
                for c in range(KC):
                    act.wait_ge(t_full, b * KC + (c + 1))
                    nc.scalar.copy(y_t[0][:, c, :], ps_t[c][:, :]).then_inc(y_hi, 1)
                for n in range(HB):
                    act.wait_ge(g_full, b * HB + (n + 1))
                    act.wait_ge(product_done, b * HB + (n + 1))
                    nc.scalar.activation(gated[n % 2][:, :], ps_g[n % 2][:, :], ACT.Silu).then_inc(silu_done, 1)
                    if n > 0:
                        upper(b, n - 1)
                    if isinstance(b, int) and n in DOWN_AT:
                        cols, _ = DOWN_AT[n]
                        act.wait_ge(down_in, 16)
                        nc.scalar.copy(w_down[0][:, cols, :], w_down_raw[:, cols, :]).then_inc(down_hi, 1)
                    if n == 5:
                        act.wait_ge(diff_ready, b + 1)
                        nc.scalar.activation(two[:, :, :], diff[:, :, :], ACT.Sigmoid).then_inc(two_ready, 1)
                        nc.scalar.activation(mix[:, :, E1], scores[:, :, E1], ACT.Sigmoid).then_inc(two_ready, 1)
                upper(b, HB - 1)
                act.wait_ge(chain, b * CHAIN_N + 7)
                for i in range(TPB):
                    tile = b * TPB + i
                    for k in range(N_SIDE):
                        fill = SIDE_FILLS[k // 2]
                        act.wait_ge(d_full, tile * D_FILLS + (fill + 1))
                        act.wait_ge(side_added, tile * ADDS + max(k, 1))
                        e = SIDE[k]
                        nc.scalar.mul(side[:, k, :], ps_d[(i * D_FILLS + fill) % 2][:, k % 2 * D:(k % 2 + 1) * D],
                                      mix[:, i, e:e + 1]).then_inc(side_scaled, 1)
                        if k % 2:
                            act.wait_ge(side_scaled, tile * N_SIDE + (k + 1))
                            act.sem_inc(side_read, 1)

            batch(0)
            with act.Fori(1, BATCH) as b:
                batch(b)

        @block.tensor
        def _(pe):
            pe.sem_inc(s_free, 1)

            def exact(out, lhs, rhs, first, final):
                for n, (i, j) in enumerate(PASSES):
                    last = nc.tensor.matmul(out, lhs(i), rhs(j), start=(first and n == 0),
                                            stop=(final and n == len(PASSES) - 1))
                return last

            with pe.Fori(0, BATCH) as b:
                for c in range(KC):
                    pe.wait_ge(y_ready, b * TPB + TPB)
                    pe.wait_ge(t_free, b * KC + (c + 1))
                    if c == 0:
                        pe.wait_ge(s_free, b + 1)
                    for i in range(TPB):
                        last = nc.tensor.transpose(ps_t[c][:, i * P:(i + 1) * P], y_tok[:, i, c * P:(c + 1) * P],
                                                   ident[:, :])
                    last.then_inc(t_full, 1)
                pe.wait_ge(t_free, b * KC + 2 * KC)
                pe.wait_ge(r_ready, 2)
                for i in range(TPB):
                    for c in range(KC):
                        last = exact(ps_t[0][:, i * NR:(i + 1) * NR], lambda m: y_t[m][:, c, i * P:(i + 1) * P],
                                     lambda m: w_r[m][:, c, :], c == 0, c == KC - 1)
                last.then_inc(s_full, 1)
                for n in range(HB):
                    pe.wait_ge(silu_done, b * HB + (n + 1))
                    for c in range(KC):
                        last = exact(ps_g[n % 2][:, :], lambda m: w_gate[m][:, c, n * H1:(n + 1) * H1],
                                     lambda m: y_t[m][:, c, :], c == 0, c == KC - 1)
                    last.then_inc(g_full, 1)
                    pe.wait_ge(product_done, b * HB + (n + 1))
                    for c in range(KC):
                        last = exact(ps_u[n % 2][:, :], lambda m: w_up[m][:, c, n * H1:(n + 1) * H1],
                                     lambda m: y_t[m][:, c, :], c == 0, c == KC - 1)
                    last.then_inc(u_full, 1)
                pe.wait_ge(down_lo, len(DOWN_AT))
                for i in range(TPB):
                    for e in range(NE):
                        at = e % 2 * D
                        if e % 2 == 0:
                            fill, tile = e // 2, b * TPB + i
                            before = (fill - 2) % D_FILLS
                            if before in SIDE_FILLS:
                                pe.wait_ge(side_read, tile * len(SIDE_FILLS) + (
                                    SIDE_FILLS.index(before) + 2 if fill >= 2 else 1))
                            else:
                                pe.wait_ge(d_free, tile * len(MAIN_FILLS) + (
                                    MAIN_FILLS.index(before) + 2 if fill >= 2 else 1))
                            pe.wait_ge(h_done, b * HB + (2 + min(HB, e + 2)))
                            o = ps_d[(i * D_FILLS + e // 2) % 2]
                        blocks = [e] if e < E1 else [E1, E1 + 1]
                        for n in blocks:
                            last = exact(o[:, at:at + D], lambda m: h[m][:, n, i * P:(i + 1) * P],
                                         lambda m: w_down[m][:, n, :], n == blocks[0], n == blocks[-1])
                        if e % 2 or e == NE - 1:
                            last.then_inc(d_full, 1)

        @block.vector
        def _(dve):
            dve.sem_inc(t_free, KC)
            dve.sem_inc(product_done, 2)
            dve.sem_inc(d_free, 1)

            def after(ins, b, c):
                ins.then_inc(chain, 1)
                dve.wait_ge(chain, b * CHAIN_N + c)

            dve.sem_inc(all_added, 1)
            def normalise(b, i):
                n = b * TPB + (PADT + i)
                xn = x[:, bass.ds(n, 1), :].rearrange("p a d -> p (a d)")
                nc.vector.tensor_scalar(y_tok[:, i, :], xn, mean[:, bass.ds(n, 1)], rstd[:, bass.ds(n, 1)],
                                        ALU.subtract, ALU.mult).then_inc(y_ready, 1)

            dve.wait_ge(consts, 1)
            for i in range(TPB):
                normalise(0, i)
            dve.wait_ge(w_in, 16)
            nc.vector.tensor_copy(w_r[0][:, :, :], w_r_raw[:, :, :]).then_inc(r_ready, 1)
            dve.wait_ge(r_ready, 1)
            nc.vector.tensor_tensor(w_r[1][:, :, :], w_r_raw[:, :, :], w_r[0][:, :, :].bitcast(F32),
                                    ALU.subtract).then_inc(r_ready, 1)
            with dve.Fori(0, BATCH) as b:
                for c in range(KC):
                    dve.wait_ge(y_hi, b * KC + (c + 1))
                    nc.vector.tensor_tensor(y_t[1][:, c, :], ps_t[c][:, :], y_t[0][:, c, :].bitcast(F32),
                                            ALU.subtract).then_inc(t_free, 1)
                dve.wait_ge(s_full, b + 1)
                nc.vector.tensor_copy(scores[:, :, :], ps_t[0][:, 0:TPB * NR].rearrange(
                    "p (i e) -> p i e", e=NR)[:, :, 0:NE]).then_inc(s_free, 1)
                held(dve, gate, s_free, b + 2)
                for i in range(TPB):
                    last = nc.vector.max(top[:, i, :], scores[:, i, 0:E1])
                last.then_inc(chain, 1)
                held(dve, gate, chain, b * CHAIN_N + 1)
                for i in range(TPB):
                    last = nc.vector.max_index(top_at[:, i, :], top[:, i, :], scores[:, i, 0:E1])
                after(last, b, 2)
                after(nc.vector.tensor_tensor(diff[:, 0, :], top[:, :, 0], top[:, :, 1], ALU.subtract), b, 3)
                nc.vector.tensor_scalar(diff[:, 1, :], diff[:, 0, :], -1.0, None, ALU.mult).then_inc(diff_ready, 1)
                after(nc.vector.tensor_copy(top_atf[:, :, :], top_at[:, :, 0:2]), b, 4)
                for k in range(2):
                    last = nc.vector.tensor_tensor(hot[:, k, :, :], numbers[:, :].unsqueeze(1).to_broadcast([P, TPB, E1]),
                                                   top_atf[:, :, k:k + 1].to_broadcast([P, TPB, E1]), ALU.is_equal)
                after(last, b, 5)
                for n in range(HB):
                    dve.wait_ge(silu_done, b * HB + (2 + n + 1))
                    dve.wait_ge(u_full, b * HB + (n + 1))
                    dve.wait_ge(h_done, b * HB + (n + 1))
                    nc.vector.tensor_tensor(product[n % 2][:, :], gated[n % 2][:, :], ps_u[n % 2][:, :],
                                            ALU.mult).then_inc(product_done, 1)
                    if n == 0:
                        dve.wait_ge(all_added, b + 1)
                    if n < TPB:
                        join.stats_of(sub, b * TPB, n)
                    if n == TPB:
                        join.sub_variance(dve, b)
                    if n == 7:
                        for i in range(TPB):
                            join.normalise_tile(dve, b, b * TPB, i)
                        join.add(dve, b, b * TPB)
                    if n == 6:
                        dve.wait_ge(two_ready, b * 2 + 2)
                        for k in range(2):
                            last = nc.vector.tensor_tensor(hot[:, k, :, :], hot[:, k, :, :],
                                                           two[:, k, :].unsqueeze(2).to_broadcast([P, TPB, E1]), ALU.mult)
                        after(last, b, 6)
                        after(nc.vector.tensor_tensor(mix[:, :, 0:E1], hot[:, 0, :, :], hot[:, 1, :, :], ALU.add), b, 7)
                for i in range(TPB):
                    acc = sub[:, bass.ds(b * TPB + (PADT + i), 1), :].rearrange("p a d -> p (a d)")
                    done = b * CHAIN_N + (7 + i * (NE - N_SIDE))
                    for k, e in enumerate(e for e in range(NE) if e not in SIDE):
                        o = ps_d[(i * D_FILLS + e // 2) % 2][:, e % 2 * D:(e % 2 + 1) * D]
                        if e % 2 == 0:
                            dve.wait_ge(d_full, (b * TPB + i) * D_FILLS + (e // 2 + 1))
                        if k == 0:
                            ins = nc.vector.tensor_scalar(acc, o, mix[:, i, e:e + 1], None, ALU.mult)
                        else:
                            dve.wait_ge(chain, done + k)
                            ins = nc.vector.scalar_tensor_tensor(acc, o, mix[:, i, e:e + 1], acc, ALU.mult, ALU.add)
                        ins.then_inc(chain, 1)
                        if e % 2 or e == NE - 1:
                            dve.wait_ge(chain, done + (k + 1))
                            dve.sem_inc(d_free, 1)
                    normalise(b + 1, i)
                dve.wait_ge(side_added, b * (TPB * ADDS) + (TPB + 1) * ADDS)
                batch = sub[:, bass.ds(b * TPB + PADT, TPB), :]
                nc.vector.tensor_tensor(batch, batch, side_sum[:, :, :], ALU.add).then_inc(all_added, 1)
            dve.wait_ge(all_added, BATCH + 1)
            join.all_on_vector(dve, BATCH, BATCH * TPB)


def program(nc, io, out):
    with ExitStack() as ctx:
        keep = keep_all(nc, ctx)
        scratch = nc.dram_tensor("scratch", (2, 2, len(Q_STACK), HD, HPG, SEQ), BF16, kind="Internal").ap()
        dispatched = nc.dram_tensor("dispatched", ((E0 + 1) * CAP, D), F32, kind="Internal").ap()
        results = nc.dram_tensor("results", (SLOTS, D), F32, kind="Internal").ap()
        keep["cleared"] = ctx.enter_context(nc.semaphore("cleared"))
        keep["x_loaded"] = [ctx.enter_context(nc.semaphore(f"x_loaded{b}")) for b in range(BATCH)]
        setup_phase(nc, keep, io["x"])
        norm_phase(nc, keep, dispatched)
        attention_phase(nc, keep, {n[3:]: a for n, a in io.items() if n.startswith("a0_")} | {"scratch": scratch}, 0)
        with ExitStack() as moe:
            route = {"gates": moe.enter_context(nc.sbuf_tensor("gates", [P, 2, TILES], F32)),
                     "get_at": moe.enter_context(nc.sbuf_tensor("get_at", [P, 2, TILES], U32))}
            w1, w2 = [{part: moe.enter_context(nc.sbuf_tensor(f"w{n}_{part}", shape, F32 if part == "raw" else F32R))
                       for part in ("raw", "hi", "lo")} for n, shape in ((1, [P, KC, FF]), (2, [P, FC, D]))]
            w = {n[3:]: a for n, a in io.items() if n.startswith("m0_")} | {"dispatched": dispatched, "results": results}
            route_phase(nc, keep, w, route, w1)
            expert_phase(nc, keep, w, w1, w2)
            combine_phase(nc, keep, w, route)
        wide = [(io[f"m1_{n}"], *(ctx.enter_context(nc.sbuf_tensor(f"w_{n}_{part}", [P, KC, HB * H1], F32R))
                                  for part in ("hi", "lo"))) for n in ("gate", "up")]
        attention_phase(nc, keep, {n[3:]: a for n, a in io.items() if n.startswith("a1_")} | {"scratch": scratch}, 1,
                        wide)
        dense_phase(nc, keep, {n[3:]: a for n, a in io.items() if n.startswith("m1_")}, wide, out)


def laid_out(inputs):
    a = {n: np.asarray(v) for n, v in inputs.items()}
    even = [2 * (d % (HD // 2)) for d in range(HD)]
    odd = [2 * (d % (HD // 2)) + 1 for d in range(HD)]
    same = list(range(HD))
    g = {n[len("L0_attn_"):]: v for n, v in a.items() if n.startswith("L0_attn_")}
    r = {"x": g["x"]}
    r["a0_x1"] = chunked(stack_columns(g["wq"], g["wk"], even))
    r["a0_x2"] = chunked(stack_columns(g["wq"], g["wk"], odd))
    r["a0_v"], r["a0_o"] = chunked(g["wv"]), chunked(g["wo"])
    r["a0_bias1"] = stack_columns(g["bq"][None], g["bk"][None], even)[0].T
    r["a0_bias2"] = stack_columns(g["bq"][None], g["bk"][None], odd)[0].T
    r["a0_bias_v"], r["a0_bias_o"] = np.tile(g["bv"][None], (P, 1)), np.tile(g["bo"][None], (P, 1))
    r["a0_rms_w"] = chunked(g["rms_w"])
    r["a0_rot1"], r["a0_rot2"] = rotation_tables()
    r["m0_g"] = chunked(a["L0_ffn_Wg"])
    r["m0_w1"], r["m0_w2"] = a["L0_ffn_w1"], a["L0_ffn_w2"]
    qkv = a["L1_attn_W_qkv"].T
    r["a1_x1"] = chunked(stack_columns(qkv[:, 0:D], qkv[:, D:2 * D], same))
    r["a1_v"], r["a1_o"] = chunked(qkv[:, 2 * D:3 * D]), chunked(a["L1_attn_W_proj"].T)
    f = {n[len("L1_ffn_"):]: v for n, v in a.items() if n.startswith("L1_ffn_")}
    r["m1_r"] = chunked(np.concatenate([f["gate_w"], f["se_gate_w"], np.zeros_like(f["se_gate_w"])]).T)
    for n in ("gate", "up"):
        r[f"m1_{n}"] = chunked(np.concatenate([f[f"w_{n}"].reshape(E1 * H1, D), f[f"sh_{n}"]]).T)
    down = np.concatenate([f["w_down"].transpose(0, 2, 1).reshape(E1 * H1, D), f["sh_down"].T])
    r["m1_down"] = chunked(down)
    return {n: np.ascontiguousarray(v) for n, v in r.items()}


def kernel(**inputs):
    import concourse.bacc as bacc
    from concourse.bass_utils import run_bass_kernel_spmd

    nc = bacc.Bacc("TRN2", target_bir_lowering=False, num_devices=1)
    arrays = {f"in_{n}": v for n, v in laid_out(inputs).items()}
    io = {n[3:]: nc.dram_tensor(n, v.shape, mybir.dt.from_np(v.dtype), kind="ExternalInput").ap()
          for n, v in arrays.items()}
    out = nc.dram_tensor("out", (BATCH, SEQ, D), F32, kind="ExternalOutput").ap()
    program(nc, io, out)
    return run_bass_kernel_spmd(nc, [arrays], core_ids=[0]).results[0]["out"]
```
